# Optimizing a Trainium2 kernel written in Bass

```python
import numpy as np
import jax
import jax.numpy as jnp

def _softmax(x, axis=-1):
    return jax.nn.softmax(x, axis=axis)
def _gelu(x):
    return jax.nn.gelu(x, approximate=True)
def _silu(x):
    return jax.nn.silu(x)
def _sigmoid(x):
    return jax.nn.sigmoid(x)
def _layernorm(x, axis=-1, eps=1e-5):
    m = jnp.mean(x, axis=axis, keepdims=True)
    v = jnp.var(x, axis=axis, keepdims=True)
    return (x - m) / jnp.sqrt(v + eps)
def _scatter_add(tgt, idx, src, axis=0):
    return tgt.at[idx].add(src)
def _segment_sum(src, seg, n):
    return jax.ops.segment_sum(src, seg, n)

kernel_name = 'mk_conv_preact_d1_conv_nhwc64_9be2af'

def setup_inputs(seed: int = 0):
    np.random.seed(seed)
    _w = jnp.asarray
    def _rec_inputs():
        import jax
        import jax.numpy as jnp
        _gk = jax.random.key(seed)
        x = -0.0001246 + 0.9999 * jax.random.normal(jax.random.fold_in(_gk, 1), (8192, 9, 9, 64), jnp.float32)
        return x
    x = _rec_inputs()
    def _L0_conv_setup():
        import jax, jax.numpy as jnp
        import numpy as np
        WS, STRIDE, GRID, HW = (3, 2, 4, 9)
        HEADS, HEAD_DIM, DIM = (4, 16, 64)
        INNER = HEADS * HEAD_DIM
        BATCH = 8192
        _RI = (np.arange(GRID) * STRIDE)[:, None] + np.arange(WS)[None, :]
        _coords = np.array([[x, y] for x in range(WS) for y in range(WS)])
        _REL = _coords[None, :, :] - _coords[:, None, :] + (WS - 1)
        key = jax.random.key(seed)
        ks = jax.random.split(key, 6)
        return {'x': jax.random.normal(ks[0], (BATCH, HW, HW, DIM), jnp.float32), 'w_qkv': jax.random.normal(ks[1], (3 * INNER, DIM), jnp.float32) * 0.05, 'pos_embedding': jax.random.normal(ks[2], (2 * WS - 1, 2 * WS - 1), jnp.float32), 'w1': jax.random.normal(ks[3], (DIM // 2, INNER), jnp.float32) * 0.05, 'b1': jnp.zeros((DIM // 2,), jnp.float32), 'ln_g': jnp.ones((DIM // 2,), jnp.float32), 'ln_b': jnp.zeros((DIM // 2,), jnp.float32), 'w2': jax.random.normal(ks[4], (DIM, DIM // 2), jnp.float32) * 0.05, 'b2': jnp.zeros((DIM,), jnp.float32)}
    _L0_conv_all = _L0_conv_setup()
    _L0_conv_in = {k: v for k, v in _L0_conv_all.items() if k in ('w_qkv', 'pos_embedding', 'w1', 'b1', 'ln_g', 'ln_b', 'w2', 'b2', )}
    del _L0_conv_all

    return {
        "x": x,
        "L0_conv_w_qkv": _L0_conv_in["w_qkv"],
        "L0_conv_pos_embedding": _L0_conv_in["pos_embedding"],
        "L0_conv_w1": _L0_conv_in["w1"],
        "L0_conv_b1": _L0_conv_in["b1"],
        "L0_conv_ln_g": _L0_conv_in["ln_g"],
        "L0_conv_ln_b": _L0_conv_in["ln_b"],
        "L0_conv_w2": _L0_conv_in["w2"],
        "L0_conv_b2": _L0_conv_in["b2"],
    }

def reference(x, L0_conv_w_qkv, L0_conv_pos_embedding, L0_conv_w1, L0_conv_b1, L0_conv_ln_g, L0_conv_ln_b, L0_conv_w2, L0_conv_b2):
    import jax
    import jax.numpy as jnp
    def _L0_conv_ref(x, w_qkv, pos_embedding, w1, b1, ln_g, ln_b, w2, b2):
        import jax, jax.numpy as jnp
        import numpy as np
        WS, STRIDE, GRID, HW = (3, 2, 4, 9)
        HEADS, HEAD_DIM, DIM = (4, 16, 64)
        INNER = HEADS * HEAD_DIM
        BATCH = 8192
        _RI = (np.arange(GRID) * STRIDE)[:, None] + np.arange(WS)[None, :]
        _coords = np.array([[x, y] for x in range(WS) for y in range(WS)])
        _REL = _coords[None, :, :] - _coords[:, None, :] + (WS - 1)
        b = x.shape[0]
        ri = jnp.asarray(_RI)
        rel0 = jnp.asarray(_REL[..., 0])
        rel1 = jnp.asarray(_REL[..., 1])
        qkv = jnp.einsum('bhwc,oc->bhwo', x, w_qkv)
        win = qkv[:, ri[:, None, :, None], ri[None, :, None, :], :]
        win = win.reshape(b, GRID * GRID, WS * WS, 3 * INNER)
        q, k, v = jnp.split(win, 3, axis=-1)

        def to_heads(t):
            return t.reshape(b, GRID * GRID, WS * WS, HEADS, HEAD_DIM).transpose(0, 3, 1, 2, 4)
        q, k, v = (to_heads(q), to_heads(k), to_heads(v))
        bias = pos_embedding[rel0, rel1]
        attn = jnp.einsum('bhwid,bhwjd->bhwij', q, k) * HEAD_DIM ** (-0.5) + bias
        attn = jax.nn.softmax(attn, axis=-1)
        out = jnp.einsum('bhwij,bhwjd->bhwid', attn, v)
        outf = out.transpose(0, 3, 1, 4, 2).reshape(b, WS * WS * INNER, GRID * GRID)
        tmp = outf.reshape(b, INNER, WS, WS, GRID, GRID).transpose(0, 4, 5, 2, 3, 1)
        canvas = jnp.zeros((b, HW, HW, INNER), out.dtype)
        canvas = canvas.at[:, ri[:, None, :, None], ri[None, :, None, :], :].add(tmp)
        h1 = jnp.einsum('bhwc,oc->bhwo', canvas, w1) + b1
        mu = jnp.mean(h1, -1, keepdims=True)
        var = jnp.var(h1, -1, keepdims=True)
        h1 = (h1 - mu) * jax.lax.rsqrt(var + 1e-05) * ln_g + ln_b
        h1 = jax.nn.gelu(h1, approximate=False)
        return jnp.einsum('bhwc,oc->bhwo', h1, w2) + b2

    def _gn(v, G=32, eps=1e-5):
        B_, H_, W_, C_ = v.shape
        g = v.reshape(B_, H_, W_, G, C_ // G)
        m = jnp.mean(g, axis=(1, 2, 4), keepdims=True)
        s = jnp.var(g, axis=(1, 2, 4), keepdims=True)
        return ((g - m) / jnp.sqrt(s + eps)).reshape(v.shape)

    def _ln_c(v, eps=1e-6):
        m = jnp.mean(v, axis=-1, keepdims=True)
        s = jnp.var(v, axis=-1, keepdims=True)
        return (v - m) / jnp.sqrt(s + eps)

    def _ln_t(v, eps=1e-5):
        m = jnp.mean(v, axis=-1, keepdims=True)
        s = jnp.var(v, axis=-1, keepdims=True)
        return (v - m) / jnp.sqrt(s + eps)

    def _to_tokens(v):
        B_, H_, W_, C_ = v.shape
        return v.reshape(B_, H_ * W_, C_)
    def _from_tokens(t, like):
        return t.reshape(like.shape)

    x = x + _L0_conv_ref(_gn(x), L0_conv_w_qkv, L0_conv_pos_embedding, L0_conv_w1, L0_conv_b1, L0_conv_ln_g, L0_conv_ln_b, L0_conv_w2, L0_conv_b2)
    return x


_drawn_inputs = setup_inputs


def setup_inputs(seed=0):
    import zlib

    import numpy as np

    out = dict(_drawn_inputs(seed))
    spreads = {'L0_conv_b1': (0.0, 0.1),
     'L0_conv_ln_g': (1.0, 0.2),
     'L0_conv_ln_b': (0.0, 0.442),
     'L0_conv_b2': (0.0, 0.1)}
    factors = {}
    for name, (base, spread) in spreads.items():
        noise = np.random.default_rng([zlib.crc32(name.encode()), seed]).standard_normal(out[name].shape)
        drawn = base * np.exp(spread * noise) if base else spread * noise
        out[name] = jnp.asarray(drawn.astype(out[name].dtype))
    for name, factor in factors.items():
        out[name] = (out[name] * factor).astype(out[name].dtype)
    return out
```

```python
import concourse.bass as bass
from concourse import mybir
from contextlib import ExitStack


def build_windowed_attention(nc, x, w_qk_t, w_v_t, pos, w1_t, b1, ln_g, ln_b, w2_t, b2, out):
    fp32 = mybir.dt.float32
    ALU = mybir.AluOpType
    ACT = mybir.ActivationFunctionType
    AX = mybir.AxisListType

    HW, WS, GRID, STRIDE = 9, 3, 4, 2
    HEADS, HD = 4, 16
    C = HEADS * HD
    HID = C // 2
    PX = HW * HW
    NW = GRID * GRID
    NT = WS * WS
    NREL = (2 * WS - 1) ** 2
    P = 128
    NBLK = x.shape[0] // P
    NG = C // 2
    GN_N = 2 * PX
    FEAT = PX * C
    BANK = 512

    def places(d):
        if d == 0:
            return 0, 1, HW
        if abs(d) == 1:
            return max(0, -d), 1, HW - 1
        return max(0, -d), STRIDE, GRID

    SLOT_PX = 36
    SLOT = SLOT_PX * C
    NSLOT = 3
    pieces = []
    for dr in range(-2, 3):
        for dc in range(-2, 3):
            n_r, n_c = places(dr)[2], places(dc)[2]
            rows = min(n_r, SLOT_PX // n_c)
            pieces += [(dr, dc, r, min(rows, n_r - r)) for r in range(0, n_r, rows)]
    pixels_of = lambda piece: piece[3] * places(piece[1])[2]
    QK_JOBS = []
    for piece in sorted(pieces, key=pixels_of, reverse=True):
        for job in QK_JOBS:
            if sum(map(pixels_of, job)) + pixels_of(piece) <= SLOT_PX:
                job.append(piece)
                break
        else:
            QK_JOBS.append([piece])
    NQK = len(QK_JOBS)
    NPIECES = len(pieces)
    GN_STEP = 4
    GN_PARTS = (C // 2 + GN_STEP - 1) // GN_STEP
    GN_FROM = NQK - 3 * GN_PARTS - 2
    QK_FOLD = [n % 5 not in (1, 3) for n in range(NQK)]
    NFOLD = sum(QK_FOLD)

    AV_JOBS = [(i, j) for i in range(NT) for j in range(0, NT, 2)]
    AV_PER_TOKEN = (NT + 1) // 2
    NAV = len(AV_JOBS)
    AV_FOLD = [j + 1 < NT and (i * 4 + j // 2) % 2 == 0 for i, j in AV_JOBS]
    NAVFOLD = sum(AV_FOLD)
    assert NAV % NSLOT == 0 and NQK % NSLOT == 0, (NAV, NQK)

    NPAIR = (PX + 1) // 2
    PAIRS_PER_BATCH = 4
    NXT = (NPAIR + PAIRS_PER_BATCH - 1) // PAIRS_PER_BATCH
    QKB = 2 * C
    NHB = (PX * HID + BANK - 1) // BANK
    TRI = 3
    NTRI = PX // TRI
    TRI_PER_BATCH = 4
    NYB = (NTRI + TRI_PER_BATCH - 1) // TRI_PER_BATCH
    YB = TRI_PER_BATCH * TRI * C
    NYSLOT = 2

    x_v = x.rearrange("(n p) r c f -> n p (r c f)", p=P)
    out_v = out.rearrange("(n p) r c f -> n p (r c f)", p=P)

    ctx = ExitStack()
    with ctx:
        def sb(name, shape):
            return ctx.enter_context(nc.sbuf_tensor(name, shape, fp32))

        def sem(name):
            return ctx.enter_context(nc.semaphore(name))

        xb = sb("xb", [P, FEAT])
        hid = xb[:, 0:PX * HID]
        hid_sq = xb[:, PX * HID:2 * PX * HID]
        qk = sb("qk", [P, PX, QKB])
        v = [sb(f"v{n}", [P, PX, C]) for n in range(2)]
        so = sb("so", [P, NW * NT * C])
        score = so[:, 0:PX * NREL * HEADS].rearrange("p (x e h) -> p x e h", e=NREL, h=HEADS)
        ec = sb("ec", [P, NT * NT * NW * HEADS])
        prob = ec[:, :].rearrange("p (i w j h) -> p i w j h", i=NT, w=NW, h=HEADS)
        canvas = ec[:, 0:FEAT].rearrange("p (x c) -> p x c", c=C)
        slot = [sb(f"slot{n}", [P, SLOT]) for n in range(NSLOT)]
        xt = [sb(f"xt{n}", [P, BANK]) for n in range(2)]
        gt = [sb(f"gt{n}", [TRI * HID + 1, BANK]) for n in range(2)]
        yb = [sb(f"yb{n}", [P, YB]) for n in range(NYSLOT)]
        top = sb("top", [P, NT, NW * HEADS])
        junk = sb("junk", [P, 2, GN_N])
        g_sum = sb("g_sum", [P, NG])
        g_neg = sb("g_neg", [P, NG])
        g_sq = sb("g_sq", [P, NG])
        g_var = sb("g_var", [P, NG])
        g_rstd = sb("g_rstd", [P, NG])
        g_off = sb("g_off", [P, NG])
        h_ss = sb("h_ss", [P, PX])
        h_var = sb("h_var", [P, PX])
        h_rstd = sb("h_rstd", [P, PX])
        minus_half = sb("minus_half", [P, PX])
        ident = sb("ident", [P, P])
        wqk = sb("wqk", [P, 2 * QKB])
        wv = sb("wv", [P, 2 * C])
        w1 = sb("w1", [P, HID])
        w1_mean = sb("w1_mean", [P, 1])
        w1_pair = sb("w1_pair", [P, 2 * HID])
        b1_row = sb("b1_row", [P, HID])
        b1_mean = sb("b1_mean", [P, 1])
        b1_mid = sb("b1_mid", [P, HID])
        w2_tri = sb("w2_tri", [TRI * HID + 1, TRI * C])
        pos_sb = sb("pos_sb", [P, NREL])
        lng = sb("lng", [TRI * HID, 1])
        lnb = sb("lnb", [TRI * HID, 1])

        ps = ctx.enter_context(nc.psum_tensor("ps", [P, 8 * BANK], fp32))

        def bank(n, count=1):
            return ps[:, n * BANK:(n + count) * BANK]

        weights_in = sem("weights_in")
        zeroed = sem("zeroed")
        ident_ready = sem("ident_ready")
        w1_steps = sem("w1_steps")
        x_in = sem("x_in")
        again_in = [sem(f"again_in{n}") for n in range(NYSLOT)]
        y_out = [sem(f"y_out{n}") for n in range(NYSLOT)]
        gn_junk = sem("gn_junk")
        gn_sums = sem("gn_sums")
        gn_neg = sem("gn_neg")
        gn_squares = sem("gn_squares")
        gn_var = sem("gn_var")
        gn_rstd = sem("gn_rstd")
        gn_off = sem("gn_off")
        x_normed = sem("x_normed")
        xt_turned = sem("xt_turned")
        xt_copied = sem("xt_copied")
        proj_done = sem("proj_done")
        proj_copied = sem("proj_copied")
        qk_multiplied = sem("qk_multiplied")
        qk_folded = sem("qk_folded")
        qk_whole_ready = sem("qk_whole_ready")
        qk_summed = sem("qk_summed")
        score_copied = sem("score_copied")
        gathered = sem("gathered")
        maxed = sem("maxed")
        shifted = sem("shifted")
        exped = sem("exped")
        den_summed = sem("den_summed")
        den_inverted = sem("den_inverted")
        prob_ready = sem("prob_ready")
        av_multiplied = sem("av_multiplied")
        av_folded = sem("av_folded")
        av_whole_ready = sem("av_whole_ready")
        av_summed = sem("av_summed")
        att_copied = sem("att_copied")
        canvas_cleared = sem("canvas_cleared")
        canvas_copied = sem("canvas_copied")
        canvas_added = sem("canvas_added")
        ct_turned = sem("ct_turned")
        ct_copied = sem("ct_copied")
        hid_done = sem("hid_done")
        hid_biased = sem("hid_biased")
        hid_squared = sem("hid_squared")
        hid_ss = sem("hid_ss")
        hid_var = sem("hid_var")
        hid_rstd = sem("hid_rstd")
        hid_scaled = sem("hid_scaled")
        ht_turned = sem("ht_turned")
        gelu_done = sem("gelu_done")
        y_done = sem("y_done")
        y_added = sem("y_added")

        NPROJ = sum((min(PAIRS_PER_BATCH, NPAIR - PAIRS_PER_BATCH * t) + 1) // 2 + 1 for t in range(NXT))
        N_ADDS = 2 * WS - 1

        def after(eng, sem_, value):
            if isinstance(value, int) and value <= 0:
                return
            eng.wait_ge(sem_, value)

        def y_uses(s):
            return len(range(s, NYB, NYSLOT))

        def pair_rows(t, m):
            return slice(C, 2 * C) if PAIRS_PER_BATCH * t + m == NPAIR - 1 else slice(0, 2 * C)

        def pair_pixels(t, m):
            return 1 if PAIRS_PER_BATCH * t + m == NPAIR - 1 else 2

        def pairs_in(t):
            return min(PAIRS_PER_BATCH, NPAIR - PAIRS_PER_BATCH * t)

        def tris_in(t):
            return min(TRI_PER_BATCH, NTRI - TRI_PER_BATCH * t)

        def window_view(buf, ki, kj):
            g = buf.rearrange("p (r c) f -> p r c f", c=HW)
            return g[:, ki:ki + STRIDE * (GRID - 1) + 1:STRIDE, kj:kj + STRIDE * (GRID - 1) + 1:STRIDE, :]

        def scores_of(i):
            ki, kj = divmod(i, WS)
            s = score.rearrange("p (r c) (a b) h -> p r c a b h", c=HW, b=2 * WS - 1)
            s = s[:, ki:ki + STRIDE * (GRID - 1) + 1:STRIDE, kj:kj + STRIDE * (GRID - 1) + 1:STRIDE]
            return s[:, :, :, WS - 1 - ki:2 * WS - 1 - ki, WS - 1 - kj:2 * WS - 1 - kj, :]

        def piece_view(buf, piece, shifted_by):
            dr, dc, r, n = piece
            (r0, rs, _), (c0, cs, nc_) = places(dr), places(dc)
            r0, c0 = r0 + rs * r + dr * shifted_by, c0 + dc * shifted_by
            g = buf.rearrange("p (r c) f -> p r c f", c=HW)
            return g[:, r0:r0 + rs * (n - 1) + 1:rs, c0:c0 + cs * (nc_ - 1) + 1:cs, :]

        block = ctx.enter_context(nc.Block())

        @block.sync
        def _(sp):
            def load_x(b):
                if isinstance(b, int) and b == 1:
                    sp.wait_ge(xt_turned, NXT)
                else:
                    sp.wait_ge(ht_turned, (b - 1) * NYB)
                sp.dma_start(xb[:, :], x_v[b]).then_inc(x_in, 16)

            sp.dma_start(xb[:, :], x_v[0]).then_inc(x_in, 16)
            for m in range(2):
                sp.wait_ge(zeroed, 4)
                rows = slice(m * C, (m + 1) * C)
                sp.dma_start(wqk[rows, m * QKB:(m + 1) * QKB], w_qk_t).then_inc(weights_in, 16)
                sp.dma_start(wv[rows, m * C:(m + 1) * C], w_v_t).then_inc(weights_in, 16)
                sp.dma_start(w1[rows, :], w1_t).then_inc(weights_in, 16)
            for m in range(TRI):
                rows = slice(m * HID, (m + 1) * HID)
                sp.dma_start(w2_tri[rows, m * C:(m + 1) * C], w2_t).then_inc(weights_in, 16)
                sp.dma_start(w2_tri[TRI * HID:TRI * HID + 1, m * C:(m + 1) * C],
                             b2.rearrange("(a n) -> a n", a=1)).then_inc(weights_in, 16)
                sp.dma_start(lng[rows, :], ln_g.rearrange("(n a) -> n a", a=1)).then_inc(weights_in, 16)
                sp.dma_start(lnb[rows, :], ln_b.rearrange("(n a) -> n a", a=1)).then_inc(weights_in, 16)
            sp.dma_start(b1_row[:, :], b1.partition_broadcast(P)).then_inc(weights_in, 16)
            sp.dma_start(pos_sb[:, :], pos.rearrange("a b -> (a b)").partition_broadcast(P)).then_inc(weights_in, 16)

            def block_io(b, follows):
                if follows:
                    load_x(b + 1)
                for t in range(NYB):
                    s, n = t % NYSLOT, tris_in(t) * TRI * C
                    after(sp, y_out[s], 16 * (b * y_uses(s) + t // NYSLOT))
                    sp.dma_start(yb[s][:, 0:n], x_v[b][:, t * YB:t * YB + n]).then_inc(again_in[s], 16)
                    if t >= 1:
                        store(b, t - 1)
                store(b, NYB - 1)

            def store(b, t):
                s, n = t % NYSLOT, tris_in(t) * TRI * C
                sp.wait_ge(y_added, b * NYB + t + 1)
                sp.dma_start(out_v[b][:, t * YB:t * YB + n], yb[s][:, 0:n]).then_inc(y_out[s], 16)

            block_io(0, True)
            with sp.Fori(1, NBLK - 1) as b:
                block_io(b, True)
            block_io(NBLK - 1, False)
            for s in range(NYSLOT):
                sp.wait_ge(y_out[s], 16 * NBLK * y_uses(s))

        @block.gpsimd
        def _(pool):
            nc.gpsimd.memset(wqk[:, :], 0.0).then_inc(zeroed, 1)
            nc.gpsimd.memset(wv[:, :], 0.0).then_inc(zeroed, 1)
            nc.gpsimd.memset(w1_pair[:, :], 0.0).then_inc(zeroed, 1)
            nc.gpsimd.memset(w2_tri[:, :], 0.0).then_inc(zeroed, 1)
            nc.gpsimd.memset(ident[:, :], 0.0).then_inc(ident_ready, 1)
            nc.gpsimd.memset(minus_half[:, :], -0.5).then_inc(zeroed, 1)
            pool.wait_ge(ident_ready, 1)
            nc.gpsimd.affine_select(out=ident[:, :], in_=ident[:, :], compare_op=ALU.not_equal, fill=1.0,
                                    base=0, pattern=[[-1, P]], channel_multiplier=1).then_inc(ident_ready, 1)

            def group_rstd(b):
                pool.wait_ge(gn_var, b + 1)
                nc.gpsimd.tensor_tensor(g_rstd[:, :], g_var[:, :], minus_half[:, 0:NG], ALU.pow).then_inc(gn_rstd, 1)

            def block_work(b, follows):
                if follows:
                    group_rstd(b + 1)
                pool.wait_ge(hid_var, b + 1)
                nc.gpsimd.tensor_tensor(h_rstd[:, :], h_var[:, :], minus_half[:, :], ALU.pow).then_inc(hid_rstd, 1)

            pool.wait_ge(zeroed, 5)
            group_rstd(0)
            block_work(0, True)
            with pool.Fori(1, NBLK - 1) as b:
                block_work(b, True)
            block_work(NBLK - 1, False)

        @block.scalar
        def _(act):
            xg = xb[:, :].rearrange("p (x g c) -> p g x c", g=NG, c=2)

            def group_norm(b, part):
                first = part % GN_PARTS * GN_STEP
                groups = range(first, min(NG, first + GN_STEP))
                if part < GN_PARTS:
                    if part == 0:
                        act.wait_ge(x_in, 16 * (b + 1))
                    for g in groups:
                        nc.scalar.activation(xg[:, g], xg[:, g], ACT.Copy,
                                             accum_out=g_sum[:, g:g + 1]).then_inc(gn_junk, 1)
                elif part < 2 * GN_PARTS:
                    if part == GN_PARTS:
                        act.wait_ge(gn_neg, b + 1)
                    for g in groups:
                        after(act, gn_junk, (2 * b + 1) * NG + g - 1)
                        nc.scalar.activation(junk[:, g % 2].rearrange("p (x c) -> p x c", c=2), xg[:, g], ACT.Square,
                                             bias=g_neg[:, g:g + 1], accum_out=g_sq[:, g:g + 1]).then_inc(gn_junk, 1)
                else:
                    if part == 2 * GN_PARTS:
                        act.wait_ge(gn_off, b + 1)
                    for g in groups:
                        ins = nc.scalar.activation(xg[:, g], xg[:, g], ACT.Identity, bias=g_off[:, g:g + 1],
                                                   scale=g_rstd[:, g:g + 1])
                    if part == 3 * GN_PARTS - 1:
                        ins.then_inc(x_normed, 1)

            def project(b, parity):
                done = b * NPROJ
                for t in range(NXT):
                    np_ = pairs_in(t)
                    act.wait_ge(xt_turned, b * NXT + t + 1)
                    if t >= 2:
                        act.wait_ge(proj_done, done - PROJ_IN[t - 1])
                    else:
                        after(act, hid_done, (b - 1) * NHB)
                    nc.scalar.activation(xt[t % 2][:, 0:np_ * P], bank(4 + t % 2)[:, 0:np_ * P],
                                         ACT.Copy).then_inc(xt_copied, 1)
                    if t == 0:
                        after(act, qk_summed, b * NQK)
                    for m in range(0, np_, 2):
                        px = 2 * (PAIRS_PER_BATCH * t + m)
                        n = min(4, PX - px)
                        done += 1
                        act.wait_ge(proj_done, done)
                        nc.scalar.activation(qk[:, px:px + n, :],
                                             bank(6 + (done - 1 - b * NPROJ) % 2)[:, 0:n * QKB].rearrange(
                                                 "p (x f) -> p x f", f=QKB),
                                             ACT.Copy).then_inc(proj_copied, 1)
                    px = 2 * PAIRS_PER_BATCH * t
                    n = min(8, PX - px)
                    done += 1
                    act.wait_ge(proj_done, done)
                    nc.scalar.activation(v[parity][:, px:px + n, :],
                                         bank(6 + (done - 1 - b * NPROJ) % 2)[:, 0:n * C].rearrange(
                                             "p (x f) -> p x f", f=C),
                                         ACT.Copy).then_inc(proj_copied, 1)

            PROJ_IN = [(pairs_in(t) + 1) // 2 + 1 for t in range(NXT)]

            def copy_scores(b, n):
                if n == 0:
                    after(act, canvas_added, b * N_ADDS)
                act.wait_ge(qk_summed, b * NQK + n + 1)
                at = 0
                for piece in QK_JOBS[n]:
                    dr, dc, _, rows = piece
                    e = (dr + WS - 1) * (2 * WS - 1) + dc + WS - 1
                    cols = pixels_of(piece)
                    ins = nc.scalar.activation(
                        piece_view(score[:, :, e, :], piece, 0),
                        bank(n % 4)[:, at * HEADS:(at + cols) * HEADS].rearrange("p (r c h) -> p r c h", r=rows, h=HEADS),
                        ACT.Identity, bias=pos_sb[:, e:e + 1], scale=HD ** -0.5)
                    at += cols
                ins.then_inc(score_copied, 1)

            def block_work(b, parity, follows):
                for n in range(NQK):
                    copy_scores(b, n)
                    if follows and 0 <= n - GN_FROM < 3 * GN_PARTS:
                        group_norm(b + 1, n - GN_FROM)
                act.wait_ge(score_copied, (b + 1) * NQK)
                after(act, ct_turned, b * NXT)
                for i in range(NT):
                    for k in range(WS):
                        ins = nc.scalar.activation(
                            prob[:, i].rearrange("p (a b) (k f) h -> p a b k (f h)", a=GRID, k=WS)[:, :, :, k],
                            scores_of(i)[:, :, :, k].rearrange("p a b f h -> p a b (f h)"), ACT.Copy)
                    ins.then_inc(gathered, 1)
                for i in range(NT):
                    act.wait_ge(shifted, b * NT + i + 1)
                    nc.scalar.activation(prob[:, i], prob[:, i], ACT.Exp).then_inc(exped, 1)
                if follows:
                    project(b + 1, 1 - parity)
                for i in range(NT):
                    act.wait_ge(av_summed, b * NAV + AV_PER_TOKEN * (i + 1))
                    for half in range(2):
                        o = so[:, half * (NW // 2) * NT * C:(half + 1) * (NW // 2) * NT * C]
                        o = o.rearrange("p (w i h d) -> p w i h d", w=NW // 2, i=NT, h=HEADS)[:, :, i]
                        s = bank(2 * (i % 2) + half).rearrange("p (w d h) -> p w h d", w=NW // 2, h=HEADS)
                        ins = nc.scalar.activation(o, s, ACT.Copy)
                    ins.then_inc(att_copied, 1)
                act.wait_ge(av_summed, (b + 1) * NAV)
                act.wait_ge(att_copied, (b + 1) * NT)
                for ki in range(WS - 1):
                    for kj in range(WS - 1):
                        nc.scalar.activation(window_view(canvas, ki, kj), folded(ki * WS + kj),
                                             ACT.Copy).then_inc(canvas_copied, 1)
                for t in range(NXT):
                    act.wait_ge(ct_turned, b * NXT + t + 1)
                    if t < 2:
                        after(act, proj_done, (b + 2 if follows else b + 1) * NPROJ)
                    else:
                        act.wait_ge(hid_done, b * NHB + (t - 2) // 2 + 1)
                    nc.scalar.activation(xt[t % 2][:, 0:pairs_in(t) * P], bank(4 + t % 2)[:, 0:pairs_in(t) * P],
                                         ACT.Copy).then_inc(ct_copied, 1)
                act.wait_ge(hid_biased, (b + 1) * NHB)
                nc.scalar.activation(hid_sq, hid, ACT.Square).then_inc(hid_squared, 1)
                for t in range(NYB):
                    n = tris_in(t) * P
                    act.wait_ge(ht_turned, b * NYB + t + 1)
                    after(act, y_done, b * NYB + t - 1)
                    nc.scalar.activation(gt[t % 2][0:TRI * HID, 0:n], bank(4 + t % 2)[0:TRI * HID, 0:n], ACT.Gelu,
                                         bias=lnb[:, :], scale=lng[:, :]).then_inc(gelu_done, 1)

            def folded(kpos):
                return so[:, :].rearrange("p (a b c k) -> p a b c k", a=GRID, b=GRID, k=NT)[:, :, :, :, kpos]

            act.wait_ge(weights_in, 16 * (3 * 2 + 4 * TRI + 2))
            act.wait_ge(zeroed, 5)
            for part in range(3 * GN_PARTS):
                group_norm(0, part)
            project(0, 0)
            block_work(0, 0, True)
            with act.Fori(1, NBLK - 1, 2) as b:
                block_work(b, 1, True)
                block_work(b + 1, 0, True)
            block_work(NBLK - 1, 1, False)

        @block.vector
        def _(dve):
            dve.wait_ge(weights_in, 16 * (3 * 2 + 4 * TRI + 2))
            dve.wait_ge(zeroed, 5)
            for n in range(2):
                nc.vector.memset(gt[n][TRI * HID:TRI * HID + 1, :], 1.0)
            nc.vector.tensor_reduce(w1_mean[:, :], w1[:, :], AX.X, ALU.add).then_inc(w1_steps, 1)
            nc.vector.tensor_reduce(b1_mean[:, :], b1_row[:, :], AX.X, ALU.add).then_inc(w1_steps, 1)
            dve.wait_ge(w1_steps, 2)
            nc.vector.tensor_scalar(w1_mean[:, :], w1_mean[:, :], 1.0 / HID, None, ALU.mult).then_inc(w1_steps, 1)
            nc.vector.tensor_scalar(b1_mean[:, :], b1_mean[:, :], 1.0 / HID, None, ALU.mult).then_inc(w1_steps, 1)
            dve.wait_ge(w1_steps, 4)
            for m in range(2):
                rows = slice(m * C, (m + 1) * C)
                nc.vector.tensor_scalar(w1_pair[rows, m * HID:(m + 1) * HID], w1[rows, :], w1_mean[rows, :], None,
                                        ALU.subtract).then_inc(w1_steps, 1)
            nc.vector.tensor_scalar(b1_mid[:, :], b1_row[:, :], b1_mean[:, :], None, ALU.subtract).then_inc(w1_steps, 1)

            def group_mean(b):
                dve.wait_ge(gn_junk, (2 * b + 1) * NG)
                nc.vector.tensor_scalar(g_neg[:, :], g_sum[:, :], -1.0 / GN_N, None, ALU.mult).then_inc(gn_neg, 1)

            def group_variance(b):
                dve.wait_ge(gn_junk, (2 * b + 2) * NG)
                nc.vector.tensor_scalar(g_var[:, :], g_sq[:, :], 1.0 / GN_N, 1e-5, ALU.mult, ALU.add).then_inc(gn_var, 1)

            def group_offset(b):
                dve.wait_ge(gn_rstd, b + 1)
                nc.vector.tensor_tensor(g_off[:, :], g_neg[:, :], g_rstd[:, :], ALU.mult).then_inc(gn_off, 1)

            def qk_products(b, n):
                if n >= NSLOT:
                    dve.wait_ge(qk_summed, b * NQK + n - NSLOT + 1)
                elif n == 0:
                    after(dve, av_summed, b * NAV)
                at = 0
                for m, piece in enumerate(QK_JOBS[n]):
                    cols = pixels_of(piece)
                    o = slot[n % NSLOT][:, at * C:(at + cols) * C].rearrange("p (r c f) -> p r c f", r=piece[3], f=C)
                    ins = nc.vector.tensor_tensor(o, piece_view(qk[:, :, 0:C], piece, 0),
                                                  piece_view(qk[:, :, C:QKB], piece, 1), ALU.mult)
                    at += cols
                ins.then_inc(qk_multiplied if QK_FOLD[n] else qk_whole_ready, 1)

            def qk_fold(b, n):
                dve.wait_ge(qk_multiplied, b * NFOLD + sum(QK_FOLD[:n + 1]))
                s = slot[n % NSLOT][:, 0:sum(map(pixels_of, QK_JOBS[n])) * C].rearrange("p (x f) -> p x f", f=C)
                nc.vector.tensor_tensor(s[:, :, 0:C // 2], s[:, :, 0:C // 2], s[:, :, C // 2:C],
                                        ALU.add).then_inc(qk_folded, 1)

            def softmax_shift(b):
                for i in range(NT + 1):
                    if i < NT:
                        dve.wait_ge(gathered, b * NT + i + 1)
                        nc.vector.tensor_reduce(top[:, i].rearrange("p (w h) -> p w h", h=HEADS),
                                                prob[:, i].rearrange("p w j h -> p w h j"), AX.X,
                                                ALU.max).then_inc(maxed, 1)
                    if i >= 1:
                        dve.wait_ge(maxed, b * NT + i)
                        m = top[:, i - 1].rearrange("p (w h) -> p w h", h=HEADS)
                        nc.vector.tensor_tensor(prob[:, i - 1], prob[:, i - 1],
                                                m[:, :, None, :].to_broadcast([P, NW, NT, HEADS]),
                                                ALU.subtract).then_inc(shifted, 1)

            def softmax_divide(b):
                THIRD = NT // 3

                def third(g):
                    i = slice(g * THIRD, (g + 1) * THIRD)
                    return prob[:, i].rearrange("p i w j h -> p (i w) j h"), top[:, i].rearrange(
                        "p i (w h) -> p (i w) h", h=HEADS)

                for g in range(3):
                    e, total = third(g)
                    dve.wait_ge(exped, b * NT + (g + 1) * THIRD)
                    nc.vector.tensor_reduce(total, e.rearrange("p w j h -> p w h j"), AX.X,
                                            ALU.add).then_inc(den_summed, 1)
                for g in range(3):
                    e, total = third(g)
                    dve.wait_ge(den_summed, 3 * b + g + 1)
                    nc.vector.reciprocal(total, total).then_inc(den_inverted, 1)
                for g in range(3):
                    e, total = third(g)
                    dve.wait_ge(den_inverted, 3 * b + g + 1)
                    nc.vector.tensor_tensor(e, e, total[:, :, None, :].to_broadcast([P, THIRD * NW, NT, HEADS]),
                                            ALU.mult).then_inc(prob_ready, 1)

            def av_products(b, n, values):
                i, j = AV_JOBS[n]
                if n >= NSLOT:
                    dve.wait_ge(av_summed, b * NAV + n - NSLOT + 1)
                elif n == 0:
                    dve.wait_ge(qk_summed, (b + 1) * NQK)
                    dve.wait_ge(prob_ready, 3 * (b + 1))
                for m in range(min(2, NT - j)):
                    o = slot[n % NSLOT][:, m * NW * C:(m + 1) * NW * C]
                    ins = nc.vector.tensor_tensor(
                        o.rearrange("p (a b f) -> p a b f", a=GRID, b=GRID),
                        prob[:, i, :, j + m, None, :].to_broadcast([P, NW, HD, HEADS]),
                        window_view(values[:, :, :], *divmod(j + m, WS)), ALU.mult)
                ins.then_inc(av_multiplied if AV_FOLD[n] else av_whole_ready, 1)

            def av_fold(b, n):
                dve.wait_ge(av_multiplied, b * NAVFOLD + sum(AV_FOLD[:n + 1]))
                s = slot[n % NSLOT]
                nc.vector.tensor_tensor(s[:, 0:NW * C], s[:, 0:NW * C], s[:, NW * C:2 * NW * C],
                                        ALU.add).then_inc(av_folded, 1)

            def fold_windows(b):
                dve.wait_ge(av_summed, (b + 1) * NAV)
                last = canvas.rearrange("p (r c) f -> p r c f", c=HW)
                nc.vector.memset(last[:, HW - 1, :, :], 0.0).then_inc(canvas_cleared, 1)
                nc.vector.memset(last[:, 0:HW - 1, HW - 1, :], 0.0).then_inc(canvas_cleared, 1)
                dve.wait_ge(canvas_copied, (b + 1) * (NT - N_ADDS))
                dve.wait_ge(canvas_cleared, 2 * (b + 1))
                later = [k for k in range(NT) if k // WS == WS - 1 or k % WS == WS - 1]
                for n, kpos in enumerate(later):
                    after(dve, canvas_added, b * N_ADDS + n)
                    src = so[:, :].rearrange("p (a b c k) -> p a b c k", a=GRID, b=GRID, k=NT)[:, :, :, :, kpos]
                    dst = window_view(canvas, *divmod(kpos, WS))
                    nc.vector.tensor_tensor(dst, dst, src, ALU.add).then_inc(canvas_added, 1)

            def block_work(b, values, follows):
                for n in range(NQK + 1):
                    if n < NQK:
                        if n == 0:
                            dve.wait_ge(proj_copied, (b + 1) * NPROJ)
                        qk_products(b, n)
                    if n >= 1 and QK_FOLD[n - 1]:
                        qk_fold(b, n - 1)
                    if follows and n == GN_FROM + GN_PARTS + 1:
                        group_mean(b + 1)
                    if follows and n == GN_FROM + 2 * GN_PARTS + 1:
                        group_variance(b + 1)
                    if follows and n == GN_FROM + 2 * GN_PARTS + 2:
                        group_offset(b + 1)
                softmax_shift(b)
                softmax_divide(b)
                for n in range(NAV + 1):
                    if n < NAV:
                        av_products(b, n, values)
                    if n >= 1 and AV_FOLD[n - 1]:
                        av_fold(b, n - 1)
                fold_windows(b)
                for t in range(NHB):
                    n = min(BANK, PX * HID - t * BANK)
                    dve.wait_ge(hid_done, b * NHB + t + 1)
                    if t == 0 and follows:
                        dve.wait_ge(xt_turned, (b + 2) * NXT)
                    nc.vector.tensor_tensor(hid[:, t * BANK:t * BANK + n].rearrange("p (x f) -> p x f", f=HID),
                                            bank(6 + t % 2)[:, 0:n].rearrange("p (x f) -> p x f", f=HID),
                                            b1_mid[:, None, :].to_broadcast([P, n // HID, HID]),
                                            ALU.add).then_inc(hid_biased, 1)
                dve.wait_ge(hid_squared, b + 1)
                nc.vector.tensor_reduce(h_ss[:, :], hid_sq.rearrange("p (x f) -> p x f", f=HID), AX.X,
                                        ALU.add).then_inc(hid_ss, 1)
                dve.wait_ge(hid_ss, b + 1)
                nc.vector.tensor_scalar(h_var[:, :], h_ss[:, :], 1.0 / HID, 1e-5, ALU.mult, ALU.add).then_inc(hid_var, 1)
                dve.wait_ge(hid_rstd, b + 1)
                h3 = hid.rearrange("p (x f) -> p x f", f=HID)
                nc.vector.tensor_tensor(h3, h3, h_rstd[:, :, None].to_broadcast([P, PX, HID]),
                                        ALU.mult).then_inc(hid_scaled, 1)
                for t in range(NYB):
                    s, n = t % NYSLOT, tris_in(t)
                    dve.wait_ge(y_done, b * NYB + t + 1)
                    dve.wait_ge(again_in[s], 16 * (b * y_uses(s) + t // NYSLOT + 1))
                    for half in range(0, n, 2):
                        w = min(2, n - half) * TRI * C
                        o = yb[s][:, half * TRI * C:half * TRI * C + w]
                        ins = nc.vector.tensor_tensor(o, o, bank(6 + half // 2)[:, 0:w], ALU.add)
                    ins.then_inc(y_added, 1)

            group_mean(0)
            group_variance(0)
            group_offset(0)
            block_work(0, v[0], True)
            with dve.Fori(1, NBLK - 1, 2) as b:
                block_work(b, v[1], True)
                block_work(b + 1, v[0], True)
            block_work(NBLK - 1, v[1], False)

        @block.tensor
        def _(pe):
            def turn(src, t, sem_):
                for m in range(pairs_in(t)):
                    at = min((PAIRS_PER_BATCH * t + m) * 2 * C, FEAT - 2 * C)
                    ins = nc.tensor.transpose(bank(4 + t % 2)[:, m * P:(m + 1) * P], src[:, at:at + 2 * C],
                                              ident[:, :])
                ins.then_inc(sem_, 1)

            def project(b):
                pe.wait_ge(x_normed, b + 1)
                after(pe, y_added, (b - 1) * NYB)
                done = b * NPROJ
                for t in range(NXT + 1):
                    if t < NXT:
                        after(pe, xt_copied, b * NXT + t - 1)
                        turn(xb, t, xt_turned)
                    if t >= 1:
                        s, np_ = t - 1, pairs_in(t - 1)
                        pe.wait_ge(xt_copied, b * NXT + s + 1)
                        for m in range(0, np_, 2):
                            after(pe, proj_copied, done - 1)
                            for k in range(m, min(m + 2, np_)):
                                rows = pair_rows(s, k)
                                n = pair_pixels(s, k) * QKB
                                ins = nc.tensor.matmul(
                                    bank(6 + (done - b * NPROJ) % 2)[:, (k - m) * 2 * QKB:(k - m) * 2 * QKB + n],
                                    xt[s % 2][rows, k * P:(k + 1) * P], wqk[rows, 2 * QKB - n:2 * QKB],
                                    start=True, stop=True)
                            ins.then_inc(proj_done, 1)
                            done += 1
                        after(pe, proj_copied, done - 1)
                        for k in range(np_):
                            rows = pair_rows(s, k)
                            n = pair_pixels(s, k) * C
                            ins = nc.tensor.matmul(bank(6 + (done - b * NPROJ) % 2)[:, k * 2 * C:k * 2 * C + n],
                                                   xt[s % 2][rows, k * P:(k + 1) * P], wv[rows, 2 * C - n:2 * C],
                                                   start=True, stop=True)
                        ins.then_inc(proj_done, 1)
                        done += 1

            def qk_sum(b, n):
                if QK_FOLD[n]:
                    pe.wait_ge(qk_folded, b * NFOLD + sum(QK_FOLD[:n + 1]))
                else:
                    pe.wait_ge(qk_whole_ready, b * (NQK - NFOLD) + n + 1 - sum(QK_FOLD[:n + 1]))
                if n >= 4:
                    pe.wait_ge(score_copied, b * NQK + n - 3)
                elif n == 0:
                    after(pe, att_copied, b * NT)
                px = sum(map(pixels_of, QK_JOBS[n]))
                terms = HD // 2 if QK_FOLD[n] else HD
                s = slot[n % NSLOT][:, 0:px * C].rearrange("p (x d h) -> p x d h", d=HD, h=HEADS)
                for d in range(terms):
                    ins = nc.tensor.matmul(bank(n % 4)[:, 0:px * HEADS], ident[:, :], s[:, :, d, :],
                                           start=(d == 0), stop=(d == terms - 1))
                ins.then_inc(qk_summed, 1)

            def av_sum(b, n):
                i, j = AV_JOBS[n]
                if AV_FOLD[n]:
                    pe.wait_ge(av_folded, b * NAVFOLD + sum(AV_FOLD[:n + 1]))
                else:
                    pe.wait_ge(av_whole_ready, b * (NAV - NAVFOLD) + n + 1 - sum(AV_FOLD[:n + 1]))
                if j == 0:
                    if i >= 2:
                        pe.wait_ge(att_copied, b * NT + i - 1)
                    elif i == 0:
                        pe.wait_ge(score_copied, (b + 1) * NQK)
                terms = 1 if AV_FOLD[n] else min(2, NT - j)
                for m in range(terms):
                    for half in range(2):
                        ins = nc.tensor.matmul(bank(2 * (i % 2) + half), ident[:, :],
                                               slot[n % NSLOT][:, m * NW * C + half * BANK:m * NW * C + (half + 1) * BANK],
                                               start=(j == 0 and m == 0), stop=(j + 2 > NT - 1 and m == terms - 1))
                ins.then_inc(av_summed, 1)

            def mlp(b, follows):
                pe.wait_ge(canvas_added, (b + 1) * N_ADDS)
                pe.wait_ge(proj_copied, (b + 2 if follows else b + 1) * NPROJ)
                for t in range(NXT + 1):
                    if t < NXT:
                        after(pe, ct_copied, b * NXT + t - 1)
                        turn(ec, t, ct_turned)
                    if t >= 1:
                        s = t - 1
                        pe.wait_ge(ct_copied, b * NXT + s + 1)
                        hb = s // 2
                        if s % 2 == 0 and hb >= 2:
                            pe.wait_ge(hid_biased, b * NHB + hb - 1)
                        for k in range(pairs_in(s)):
                            rows = pair_rows(s, k)
                            n = pair_pixels(s, k) * HID
                            at = ((s % 2) * PAIRS_PER_BATCH + k) * 2 * HID
                            ins = nc.tensor.matmul(bank(6 + hb % 2)[:, at:at + n],
                                                   xt[s % 2][rows, k * P:(k + 1) * P],
                                                   w1_pair[rows, 2 * HID - n:2 * HID],
                                                   start=True, stop=True)
                        if s % 2 == 1 or s == NXT - 1:
                            ins.then_inc(hid_done, 1)
                pe.wait_ge(hid_scaled, b + 1)
                for t in range(NYB + 1):
                    if t < NYB:
                        after(pe, gelu_done, b * NYB + t - 1)
                        for m in range(tris_in(t)):
                            at = (TRI_PER_BATCH * t + m) * TRI * HID
                            ins = nc.tensor.transpose(bank(4 + t % 2)[0:TRI * HID, m * P:(m + 1) * P],
                                                      hid[:, at:at + TRI * HID], ident[:, :])
                        ins.then_inc(ht_turned, 1)
                    if t >= 1:
                        s = t - 1
                        pe.wait_ge(gelu_done, b * NYB + s + 1)
                        if s == 0:
                            pe.wait_ge(hid_biased, (b + 1) * NHB)
                        else:
                            pe.wait_ge(y_added, b * NYB + s)
                        for m in range(tris_in(s)):
                            ins = nc.tensor.matmul(bank(6 + m // 2)[:, (m % 2) * TRI * C:(m % 2 + 1) * TRI * C],
                                                   gt[s % 2][:, m * P:(m + 1) * P], w2_tri[:, :], start=True, stop=True)
                        ins.then_inc(y_done, 1)

            def block_work(b, follows):
                for n in range(NQK):
                    qk_sum(b, n)
                if follows:
                    project(b + 1)
                for n in range(NAV):
                    av_sum(b, n)
                mlp(b, follows)

            pe.wait_ge(ident_ready, 2)
            pe.wait_ge(weights_in, 16 * (3 * 2 + 4 * TRI + 2))
            pe.wait_ge(w1_steps, 7)
            project(0)
            block_work(0, True)
            with pe.Fori(1, NBLK - 1) as b:
                block_work(b, True)
            block_work(NBLK - 1, False)


def kernel(x, L0_conv_w_qkv, L0_conv_pos_embedding, L0_conv_w1, L0_conv_b1, L0_conv_ln_g, L0_conv_ln_b, L0_conv_w2,
           L0_conv_b2):
    import numpy as np
    import concourse.bacc as bacc
    from concourse.bass_utils import run_bass_kernel_spmd

    HEADS, HD = 4, 16
    C = HEADS * HD
    w = np.asarray(L0_conv_w_qkv).reshape(3, HEADS, HD, C).transpose(3, 0, 2, 1).reshape(C, 3 * C)
    arrays = {
        "x": np.ascontiguousarray(x),
        "w_qk_t": np.ascontiguousarray(w[:, :2 * C]),
        "w_v_t": np.ascontiguousarray(w[:, 2 * C:]),
        "pos": np.ascontiguousarray(L0_conv_pos_embedding),
        "w1_t": np.ascontiguousarray(np.asarray(L0_conv_w1).T),
        "b1": np.ascontiguousarray(L0_conv_b1),
        "ln_g": np.ascontiguousarray(L0_conv_ln_g),
        "ln_b": np.ascontiguousarray(L0_conv_ln_b),
        "w2_t": np.ascontiguousarray(np.asarray(L0_conv_w2).T),
        "b2": np.ascontiguousarray(L0_conv_b2),
    }
    nc = bacc.Bacc("TRN2", target_bir_lowering=False, num_devices=1)
    args = [nc.dram_tensor(f"in_{n}", a.shape, mybir.dt.float32, kind="ExternalInput").ap() for n, a in arrays.items()]
    out = nc.dram_tensor("out_y", arrays["x"].shape, mybir.dt.float32, kind="ExternalOutput").ap()
    build_windowed_attention(nc, *args, out)
    r = run_bass_kernel_spmd(nc, [{f"in_{n}": a for n, a in arrays.items()}], core_ids=[0])
    return r.results[0]["out_y"]
```

```python
import concourse.bass as bass
from concourse import mybir
from contextlib import ExitStack


def build_windowed_attention(nc, x, w_qk_t, w_v_t, pos, w1_t, b1, ln_g, ln_b, w2_t, b2, out):
    fp32 = mybir.dt.float32
    ALU = mybir.AluOpType
    ACT = mybir.ActivationFunctionType
    AX = mybir.AxisListType

    HW, WS, GRID, STRIDE = 9, 3, 4, 2
    HEADS, HD = 4, 16
    C = HEADS * HD
    HID = C // 2
    PX = HW * HW
    NW = GRID * GRID
    NT = WS * WS
    NREL = (2 * WS - 1) ** 2
    P = 128
    NBLK = x.shape[0] // P
    NG = C // 2
    GN_N = 2 * PX
    FEAT = PX * C
    BANK = 512

    def places(d):
        if d == 0:
            return 0, 1, HW
        if abs(d) == 1:
            return max(0, -d), 1, HW - 1
        return max(0, -d), STRIDE, GRID

    SLOT_PX = 36
    SLOT = SLOT_PX * C
    NSLOT = 3
    pieces = []
    for dr in range(-2, 3):
        for dc in range(-2, 3):
            n_r, n_c = places(dr)[2], places(dc)[2]
            rows = min(n_r, SLOT_PX // n_c)
            pieces += [(dr, dc, r, min(rows, n_r - r)) for r in range(0, n_r, rows)]
    pixels_of = lambda piece: piece[3] * places(piece[1])[2]
    QK_JOBS = []
    for piece in sorted(pieces, key=pixels_of, reverse=True):
        for job in QK_JOBS:
            if sum(map(pixels_of, job)) + pixels_of(piece) <= SLOT_PX:
                job.append(piece)
                break
        else:
            QK_JOBS.append([piece])
    NQK = len(QK_JOBS)
    NPIECES = len(pieces)
    GN_STEP = 4
    GN_PARTS = (C // 2 + GN_STEP - 1) // GN_STEP
    QK_FOLD = [n % 5 not in (1, 3) for n in range(NQK)]
    NFOLD = sum(QK_FOLD)

    AV_JOBS = [(i, j) for i in range(NT) for j in range(0, NT, 2)]
    AV_PER_TOKEN = (NT + 1) // 2
    NAV = len(AV_JOBS)
    AV_FOLD = [j + 1 < NT for i, j in AV_JOBS]
    NAVFOLD = sum(AV_FOLD)
    assert NAV % NSLOT == 0 and NQK % NSLOT == 0, (NAV, NQK)

    NPAIR = (PX + 1) // 2
    PAIRS_PER_BATCH = 4
    NXT = (NPAIR + PAIRS_PER_BATCH - 1) // PAIRS_PER_BATCH
    QKB = 2 * C
    NHB = (PX * HID + BANK - 1) // BANK
    TRI = 3
    NTRI = PX // TRI
    TRI_PER_BATCH = 4
    NYB = (NTRI + TRI_PER_BATCH - 1) // TRI_PER_BATCH
    YB = TRI_PER_BATCH * TRI * C
    NYSLOT = 2

    x_v = x.rearrange("(n p) r c f -> n p (r c f)", p=P)
    out_v = out.rearrange("(n p) r c f -> n p (r c f)", p=P)

    ctx = ExitStack()
    with ctx:
        def sb(name, shape):
            return ctx.enter_context(nc.sbuf_tensor(name, shape, fp32))

        def sem(name):
            return ctx.enter_context(nc.semaphore(name))

        xb = sb("xb", [P, FEAT])
        qk = sb("qk", [P, PX, QKB])
        v = [sb(f"v{n}", [P, PX, C]) for n in range(2)]
        so = sb("so", [P, NW * NT * C])
        score = so[:, 0:PX * NREL * HEADS].rearrange("p (x e h) -> p x e h", e=NREL, h=HEADS)
        ec = sb("ec", [P, NT * NT * NW * HEADS])
        prob = ec[:, :].rearrange("p (i w j h) -> p i w j h", i=NT, w=NW, h=HEADS)
        canvas = ec[:, 0:FEAT].rearrange("p (x c) -> p x c", c=C)
        hid = ec[:, 0:PX * HID]
        hid_sq = ec[:, PX * HID:2 * PX * HID]
        slot = [sb(f"slot{n}", [P, SLOT]) for n in range(NSLOT)]
        xt = [sb(f"xt{n}", [P, BANK]) for n in range(2)]
        gt = [sb(f"gt{n}", [TRI * HID + 1, BANK]) for n in range(2)]
        yb = [sb(f"yb{n}", [P, YB]) for n in range(NYSLOT)]
        top = sb("top", [P, NT, NW * HEADS])
        junk = so[:, PX * NREL * HEADS:PX * NREL * HEADS + 2 * GN_N].rearrange("p (a f) -> p a f", a=2)
        g_sum = sb("g_sum", [P, NG])
        g_neg = sb("g_neg", [P, NG])
        g_sq = sb("g_sq", [P, NG])
        g_var = sb("g_var", [P, NG])
        g_rstd = sb("g_rstd", [P, NG])
        g_off = sb("g_off", [P, NG])
        h_ss = sb("h_ss", [P, PX])
        h_var = sb("h_var", [P, PX])
        h_rstd = sb("h_rstd", [P, PX])
        minus_half = sb("minus_half", [P, PX])
        ident = sb("ident", [P, P])
        wqk = sb("wqk", [P, 2 * QKB])
        wv = sb("wv", [P, 2 * C])
        w1 = sb("w1", [P, HID])
        w1_mean = sb("w1_mean", [P, 1])
        w1_pair = sb("w1_pair", [P, 4 * HID])
        b1_row = sb("b1_row", [P, HID])
        b1_mean = sb("b1_mean", [P, 1])
        b1_mid = sb("b1_mid", [P, HID])
        w2_tri = sb("w2_tri", [TRI * HID + 1, TRI * C])
        pos_sb = sb("pos_sb", [P, NREL])
        lng = sb("lng", [TRI * HID, 1])
        lnb = sb("lnb", [TRI * HID, 1])

        ps = ctx.enter_context(nc.psum_tensor("ps", [P, 8 * BANK], fp32))

        PROB_BANK, ATT_BANK = (0, 1), (2, 6)
        TURN_BANK, PROJ_BANK = 4, 5
        PJ = BANK // (NW * HEADS)

        def bank(n, count=1):
            return ps[:, n * BANK:(n + count) * BANK]

        weights_in = sem("weights_in")
        zeroed = sem("zeroed")
        ident_ready = sem("ident_ready")
        w1_steps = sem("w1_steps")
        x_in = sem("x_in")
        again_in = [sem(f"again_in{n}") for n in range(NYSLOT)]
        y_out = [sem(f"y_out{n}") for n in range(NYSLOT)]
        gn_junk = sem("gn_junk")
        gn_sums = sem("gn_sums")
        gn_neg = sem("gn_neg")
        gn_squares = sem("gn_squares")
        gn_var = sem("gn_var")
        gn_rstd = sem("gn_rstd")
        gn_off = sem("gn_off")
        x_normed = sem("x_normed")
        xt_turned = sem("xt_turned")
        xt_copied = sem("xt_copied")
        proj_done = sem("proj_done")
        proj_copied = sem("proj_copied")
        qk_multiplied = sem("qk_multiplied")
        qk_folded = sem("qk_folded")
        qk_whole_ready = sem("qk_whole_ready")
        qk_summed = sem("qk_summed")
        score_copied = sem("score_copied")
        gathered = sem("gathered")
        maxed = sem("maxed")
        shifted = sem("shifted")
        exped = sem("exped")
        den_summed = sem("den_summed")
        den_inverted = sem("den_inverted")
        prob_ready = sem("prob_ready")
        av_multiplied = sem("av_multiplied")
        av_folded = sem("av_folded")
        av_whole_ready = sem("av_whole_ready")
        av_summed = sem("av_summed")
        att_copied = sem("att_copied")
        canvas_cleared = sem("canvas_cleared")
        canvas_copied = sem("canvas_copied")
        canvas_added = sem("canvas_added")
        ct_turned = sem("ct_turned")
        ct_copied = sem("ct_copied")
        hid_done = sem("hid_done")
        hid_biased = sem("hid_biased")
        hid_squared = sem("hid_squared")
        hid_ss = sem("hid_ss")
        hid_var = sem("hid_var")
        hid_rstd = sem("hid_rstd")
        hid_scaled = sem("hid_scaled")
        ht_turned = sem("ht_turned")
        gelu_done = sem("gelu_done")
        y_done = sem("y_done")
        y_added = sem("y_added")

        STEPS = [("turn", 0, 0)]
        for t in range(NXT):
            if t + 1 < NXT:
                STEPS.append(("turn", t + 1, 0))
            STEPS += [("qk", t, m) for m in range(0, min(PAIRS_PER_BATCH, NPAIR - PAIRS_PER_BATCH * t), 2)]
            STEPS.append(("v", t, 0))
        STEPS_EARLY = 4
        STEPS_SOFTMAX = 10
        projections = [k for k, step in enumerate(STEPS) if step[0] != "turn"]
        NPROJ = sum((min(PAIRS_PER_BATCH, NPAIR - PAIRS_PER_BATCH * t) + 1) // 2 + 1 for t in range(NXT))
        assert NPROJ == len(projections) and len(STEPS) - STEPS_SOFTMAX <= NAV
        N_ADDS = 2 * WS - 1

        def projected(k):
            return sum(p < k for p in projections)

        TURN_AT = 3
        BIAS_AT = TURN_AT + 4
        SQUARE_AT = BIAS_AT + NHB - 1
        SUM_AT = SQUARE_AT + 3
        TRI_AT = SUM_AT + 3
        OUT_AT = TRI_AT + 5
        MLP_STEPS = OUT_AT + 2 * NYB
        GN_AT = (0, GN_PARTS + 2, 2 * GN_PARTS + 5)
        GN_MEAN_AT, GN_VAR_AT = GN_AT[1] + 1, GN_AT[2]
        assert GN_AT[2] + GN_PARTS <= NQK

        def after(eng, sem_, value):
            if isinstance(value, int) and value <= 0:
                return
            eng.wait_ge(sem_, value)

        def y_uses(s):
            return len(range(s, NYB, NYSLOT))

        def pair_rows(t, m):
            return slice(C, 2 * C) if PAIRS_PER_BATCH * t + m == NPAIR - 1 else slice(0, 2 * C)

        def pair_pixels(t, m):
            return 1 if PAIRS_PER_BATCH * t + m == NPAIR - 1 else 2

        def pairs_in(t):
            return min(PAIRS_PER_BATCH, NPAIR - PAIRS_PER_BATCH * t)

        def tris_in(t):
            return min(TRI_PER_BATCH, NTRI - TRI_PER_BATCH * t)

        def window_view(buf, ki, kj):
            g = buf.rearrange("p (r c) f -> p r c f", c=HW)
            return g[:, ki:ki + STRIDE * (GRID - 1) + 1:STRIDE, kj:kj + STRIDE * (GRID - 1) + 1:STRIDE, :]

        def scores_of(i):
            ki, kj = divmod(i, WS)
            s = score.rearrange("p (r c) (a b) h -> p r c a b h", c=HW, b=2 * WS - 1)
            s = s[:, ki:ki + STRIDE * (GRID - 1) + 1:STRIDE, kj:kj + STRIDE * (GRID - 1) + 1:STRIDE]
            return s[:, :, :, WS - 1 - ki:2 * WS - 1 - ki, WS - 1 - kj:2 * WS - 1 - kj, :]

        def piece_view(buf, piece, shifted_by):
            dr, dc, r, n = piece
            (r0, rs, _), (c0, cs, nc_) = places(dr), places(dc)
            r0, c0 = r0 + rs * r + dr * shifted_by, c0 + dc * shifted_by
            g = buf.rearrange("p (r c) f -> p r c f", c=HW)
            return g[:, r0:r0 + rs * (n - 1) + 1:rs, c0:c0 + cs * (nc_ - 1) + 1:cs, :]

        block = ctx.enter_context(nc.Block())

        @block.sync
        def _(sp):
            def load_x(b):
                sp.wait_ge(xt_turned, b * NXT)
                sp.dma_start(xb[:, :], x_v[b]).then_inc(x_in, 16)

            sp.dma_start(xb[:, :], x_v[0]).then_inc(x_in, 16)
            for m in range(2):
                sp.wait_ge(zeroed, 4)
                rows = slice(m * C, (m + 1) * C)
                sp.dma_start(wqk[rows, m * QKB:(m + 1) * QKB], w_qk_t).then_inc(weights_in, 16)
                sp.dma_start(wv[rows, m * C:(m + 1) * C], w_v_t).then_inc(weights_in, 16)
                sp.dma_start(w1[rows, :], w1_t).then_inc(weights_in, 16)
            for m in range(TRI):
                rows = slice(m * HID, (m + 1) * HID)
                sp.dma_start(w2_tri[rows, m * C:(m + 1) * C], w2_t).then_inc(weights_in, 16)
                sp.dma_start(w2_tri[TRI * HID:TRI * HID + 1, m * C:(m + 1) * C],
                             b2.rearrange("(a n) -> a n", a=1)).then_inc(weights_in, 16)
                sp.dma_start(lng[rows, :], ln_g.rearrange("(n a) -> n a", a=1)).then_inc(weights_in, 16)
                sp.dma_start(lnb[rows, :], ln_b.rearrange("(n a) -> n a", a=1)).then_inc(weights_in, 16)
            sp.dma_start(b1_row[:, :], b1.partition_broadcast(P)).then_inc(weights_in, 16)
            sp.dma_start(pos_sb[:, :], pos.rearrange("a b -> (a b)").partition_broadcast(P)).then_inc(weights_in, 16)

            def block_io(b, follows):
                if follows:
                    load_x(b + 2)
                for t in range(NYB):
                    s, n = t % NYSLOT, tris_in(t) * TRI * C
                    after(sp, y_out[s], 16 * (b * y_uses(s) + t // NYSLOT))
                    sp.dma_start(yb[s][:, 0:n], x_v[b][:, t * YB:t * YB + n]).then_inc(again_in[s], 16)
                    if t >= 1:
                        store(b, t - 1)
                store(b, NYB - 1)

            def store(b, t):
                s, n = t % NYSLOT, tris_in(t) * TRI * C
                sp.wait_ge(y_added, b * NYB + t + 1)
                sp.dma_start(out_v[b][:, t * YB:t * YB + n], yb[s][:, 0:n]).then_inc(y_out[s], 16)

            load_x(1)
            block_io(0, True)
            with sp.Fori(1, NBLK - 2) as b:
                block_io(b, True)
            block_io(NBLK - 2, False)
            block_io(NBLK - 1, False)
            for s in range(NYSLOT):
                sp.wait_ge(y_out[s], 16 * NBLK * y_uses(s))

        @block.gpsimd
        def _(pool):
            nc.gpsimd.memset(wqk[:, :], 0.0).then_inc(zeroed, 1)
            nc.gpsimd.memset(wv[:, :], 0.0).then_inc(zeroed, 1)
            nc.gpsimd.memset(w1_pair[:, :], 0.0).then_inc(zeroed, 1)
            nc.gpsimd.memset(w2_tri[:, :], 0.0).then_inc(zeroed, 1)
            nc.gpsimd.memset(ident[:, :], 0.0).then_inc(ident_ready, 1)
            nc.gpsimd.memset(minus_half[:, :], -0.5).then_inc(zeroed, 1)
            pool.wait_ge(ident_ready, 1)
            nc.gpsimd.affine_select(out=ident[:, :], in_=ident[:, :], compare_op=ALU.not_equal, fill=1.0,
                                    base=0, pattern=[[-1, P]], channel_multiplier=1).then_inc(ident_ready, 1)

            def group_rstd(b):
                pool.wait_ge(gn_var, b + 1)
                nc.gpsimd.tensor_tensor(g_rstd[:, :], g_var[:, :], minus_half[:, 0:NG], ALU.pow).then_inc(gn_rstd, 1)

            def pixel_rstd(b):
                pool.wait_ge(hid_var, b + 1)
                nc.gpsimd.tensor_tensor(h_rstd[:, :], h_var[:, :], minus_half[:, :], ALU.pow).then_inc(hid_rstd, 1)

            def add_pairs(b):
                for n in range(NAV):
                    if AV_FOLD[n]:
                        pool.wait_ge(av_multiplied, b * NAVFOLD + sum(AV_FOLD[:n + 1]))
                        s = slot[n % NSLOT]
                        nc.gpsimd.tensor_tensor(s[:, 0:NW * C], s[:, 0:NW * C], s[:, NW * C:2 * NW * C],
                                                ALU.add).then_inc(av_folded, 1)

            def block_work(b, preceded, follows):
                if preceded:
                    pixel_rstd(b - 1)
                if follows:
                    group_rstd(b + 1)
                add_pairs(b)

            pool.wait_ge(zeroed, 5)
            group_rstd(0)
            block_work(0, False, True)
            with pool.Fori(1, NBLK - 1) as b:
                block_work(b, True, True)
            block_work(NBLK - 1, True, False)
            pixel_rstd(NBLK - 1)

        @block.scalar
        def _(act):
            xg = xb[:, :].rearrange("p (x g c) -> p g x c", g=NG, c=2)

            def group_norm(b, part):
                first = part % GN_PARTS * GN_STEP
                groups = range(first, min(NG, first + GN_STEP))
                if part < GN_PARTS:
                    if part == 0:
                        act.wait_ge(x_in, 16 * (b + 1))
                    for g in groups:
                        nc.scalar.activation(xg[:, g], xg[:, g], ACT.Copy,
                                             accum_out=g_sum[:, g:g + 1]).then_inc(gn_junk, 1)
                elif part < 2 * GN_PARTS:
                    if part == GN_PARTS:
                        act.wait_ge(gn_neg, b + 1)
                    for g in groups:
                        after(act, gn_junk, (2 * b + 1) * NG + g - 1)
                        nc.scalar.activation(junk[:, g % 2].rearrange("p (x c) -> p x c", c=2), xg[:, g], ACT.Square,
                                             bias=g_neg[:, g:g + 1], accum_out=g_sq[:, g:g + 1]).then_inc(gn_junk, 1)
                else:
                    if part == 2 * GN_PARTS:
                        act.wait_ge(gn_off, b + 1)
                    for g in groups:
                        ins = nc.scalar.activation(xg[:, g], xg[:, g], ACT.Identity, bias=g_off[:, g:g + 1],
                                                   scale=g_rstd[:, g:g + 1])
                    if part == 3 * GN_PARTS - 1:
                        ins.then_inc(x_normed, 1)

            def project(b, parity, k):
                kind, t, m = STEPS[k]
                if kind == "turn":
                    act.wait_ge(xt_turned, b * NXT + t + 1)
                    if t >= 2:
                        act.wait_ge(proj_done, b * NPROJ + projected(STEPS.index(("v", t - 2, 0)) + 1))
                    else:
                        after(act, hid_done, (b - 1) * NHB)
                    nc.scalar.activation(xt[t % 2][:, 0:pairs_in(t) * P], bank(TURN_BANK)[:, 0:pairs_in(t) * P],
                                         ACT.Copy).then_inc(xt_copied, 1)
                    return
                act.wait_ge(proj_done, b * NPROJ + projected(k + 1))
                if kind == "qk":
                    px = 2 * (PAIRS_PER_BATCH * t + m)
                    n, width, dst = min(4, PX - px), QKB, qk
                else:
                    px = 2 * PAIRS_PER_BATCH * t
                    n, width, dst = min(8, PX - px), C, v[parity]
                nc.scalar.activation(dst[:, px:px + n, :],
                                     bank(PROJ_BANK)[:, 0:n * width].rearrange("p (x f) -> p x f", f=width),
                                     ACT.Copy).then_inc(proj_copied, 1)

            def copy_scores(b, n):
                if n == 0:
                    after(act, canvas_added, b * N_ADDS)
                act.wait_ge(qk_summed, b * NQK + n + 1)
                at = 0
                for piece in QK_JOBS[n]:
                    dr, dc, _, rows = piece
                    e = (dr + WS - 1) * (2 * WS - 1) + dc + WS - 1
                    cols = pixels_of(piece)
                    ins = nc.scalar.activation(
                        piece_view(score[:, :, e, :], piece, 0),
                        bank(n % 4)[:, at * HEADS:(at + cols) * HEADS].rearrange("p (r c h) -> p r c h", r=rows, h=HEADS),
                        ACT.Identity, bias=pos_sb[:, e:e + 1], scale=HD ** -0.5)
                    at += cols
                ins.then_inc(score_copied, 1)

            def mlp(b, n, follows):
                if TURN_AT <= n < TURN_AT + NHB:
                    for t in range(2 * (n - TURN_AT), min(2 * (n - TURN_AT) + 2, NXT)):
                        act.wait_ge(ct_turned, b * NXT + t + 1)
                        if t < 2:
                            act.wait_ge(proj_done, (b + 2 if follows else b + 1) * NPROJ)
                        else:
                            act.wait_ge(hid_done, b * NHB + (t - 2) // 2 + 1)
                        nc.scalar.activation(xt[t % 2][:, 0:pairs_in(t) * P], bank(4 + t % 2)[:, 0:pairs_in(t) * P],
                                             ACT.Copy).then_inc(ct_copied, 1)
                if n == SQUARE_AT:
                    act.wait_ge(hid_biased, (b + 1) * NHB)
                    nc.scalar.activation(hid_sq, hid, ACT.Square).then_inc(hid_squared, 1)
                if (n - TRI_AT) % 2 == 0 and 0 <= (n - TRI_AT) // 2 < NYB:
                    t = (n - TRI_AT) // 2
                    w = tris_in(t) * P
                    act.wait_ge(ht_turned, b * NYB + t + 1)
                    if t >= 2:
                        act.wait_ge(y_done, b * NYB + t - 1)
                    nc.scalar.activation(gt[t % 2][0:TRI * HID, 0:w], bank(4 + t % 2)[0:TRI * HID, 0:w], ACT.Gelu,
                                         bias=lnb[:, :], scale=lng[:, :]).then_inc(gelu_done, 1)

            def block_work(b, parity, preceded, follows):
                for n in range(NQK):
                    copy_scores(b, n)
                    if preceded:
                        mlp(b - 1, n, True)
                    for p, start in enumerate(GN_AT):
                        if follows and start <= n < start + GN_PARTS:
                            group_norm(b + 1, p * GN_PARTS + n - start)
                if preceded:
                    for n in range(NQK, MLP_STEPS):
                        mlp(b - 1, n, True)
                act.wait_ge(score_copied, (b + 1) * NQK)
                after(act, ht_turned, b * NYB)
                for i in range(NT):
                    for k in range(WS):
                        ins = nc.scalar.activation(
                            prob[:, i].rearrange("p (a b) (k f) h -> p a b k (f h)", a=GRID, k=WS)[:, :, :, k],
                            scores_of(i)[:, :, :, k].rearrange("p a b f h -> p a b (f h)"), ACT.Copy)
                    ins.then_inc(gathered, 1)
                if follows:
                    for k in range(STEPS_EARLY):
                        project(b + 1, 1 - parity, k)
                for i in range(NT):
                    act.wait_ge(shifted, b * NT + i + 1)
                    nc.scalar.activation(prob[:, i], prob[:, i], ACT.Exp).then_inc(exped, 1)
                if follows:
                    for k in range(STEPS_EARLY, STEPS_SOFTMAX):
                        project(b + 1, 1 - parity, k)
                for n, (i, j) in enumerate(AV_JOBS):
                    if follows and STEPS_SOFTMAX + n < len(STEPS):
                        project(b + 1, 1 - parity, STEPS_SOFTMAX + n)
                    if (n + 1) % AV_PER_TOKEN:
                        continue
                    act.wait_ge(av_summed, b * NAV + n + 1)
                    o = so[:, :].rearrange("p (w i h d) -> p w i h d", w=NW, i=NT, h=HEADS)[:, :, i]
                    s = bank(ATT_BANK[i % 2], 2).rearrange("p (w d h) -> p w h d", w=NW, h=HEADS)
                    for half in range(2):
                        w = slice(half * (NW // 2), (half + 1) * (NW // 2))
                        ins = nc.scalar.activation(o[:, w], s[:, w], ACT.Copy)
                    ins.then_inc(att_copied, 1)
                act.wait_ge(att_copied, (b + 1) * NT)
                for ki in range(WS - 1):
                    for kj in range(WS - 1):
                        nc.scalar.activation(window_view(canvas, ki, kj), folded(ki * WS + kj),
                                             ACT.Copy).then_inc(canvas_copied, 1)

            def folded(kpos):
                return so[:, :].rearrange("p (a b c k) -> p a b c k", a=GRID, b=GRID, k=NT)[:, :, :, :, kpos]

            act.wait_ge(weights_in, 16 * (3 * 2 + 4 * TRI + 2))
            act.wait_ge(zeroed, 5)
            for part in range(3 * GN_PARTS):
                group_norm(0, part)
            for k in range(len(STEPS)):
                project(0, 0, k)
            block_work(0, 0, False, True)
            with act.Fori(1, NBLK - 1, 2) as b:
                block_work(b, 1, True, True)
                block_work(b + 1, 0, True, True)
            block_work(NBLK - 1, 1, True, False)
            for n in range(MLP_STEPS):
                mlp(NBLK - 1, n, False)

        @block.vector
        def _(dve):
            dve.wait_ge(weights_in, 16 * (3 * 2 + 4 * TRI + 2))
            dve.wait_ge(zeroed, 5)
            for n in range(2):
                nc.vector.memset(gt[n][TRI * HID:TRI * HID + 1, :], 1.0)
            nc.vector.tensor_reduce(w1_mean[:, :], w1[:, :], AX.X, ALU.add).then_inc(w1_steps, 1)
            nc.vector.tensor_reduce(b1_mean[:, :], b1_row[:, :], AX.X, ALU.add).then_inc(w1_steps, 1)
            dve.wait_ge(w1_steps, 2)
            nc.vector.tensor_scalar(w1_mean[:, :], w1_mean[:, :], 1.0 / HID, None, ALU.mult).then_inc(w1_steps, 1)
            nc.vector.tensor_scalar(b1_mean[:, :], b1_mean[:, :], 1.0 / HID, None, ALU.mult).then_inc(w1_steps, 1)
            dve.wait_ge(w1_steps, 4)
            for m in range(2):
                rows = slice(m * C, (m + 1) * C)
                nc.vector.tensor_scalar(w1_pair[rows, m * HID:(m + 1) * HID], w1[rows, :], w1_mean[rows, :], None,
                                        ALU.subtract).then_inc(w1_steps, 1)
            nc.vector.tensor_scalar(b1_mid[:, :], b1_row[:, :], b1_mean[:, :], None, ALU.subtract).then_inc(w1_steps, 1)

            def group_mean(b):
                dve.wait_ge(gn_junk, (2 * b + 1) * NG)
                nc.vector.tensor_scalar(g_neg[:, :], g_sum[:, :], -1.0 / GN_N, None, ALU.mult).then_inc(gn_neg, 1)

            def group_variance(b):
                dve.wait_ge(gn_junk, (2 * b + 2) * NG)
                nc.vector.tensor_scalar(g_var[:, :], g_sq[:, :], 1.0 / GN_N, 1e-5, ALU.mult, ALU.add).then_inc(gn_var, 1)

            def group_offset(b):
                dve.wait_ge(gn_rstd, b + 1)
                nc.vector.tensor_tensor(g_off[:, :], g_neg[:, :], g_rstd[:, :], ALU.mult).then_inc(gn_off, 1)

            def qk_products(b, n):
                if n >= NSLOT:
                    dve.wait_ge(qk_summed, b * NQK + n - NSLOT + 1)
                else:
                    after(dve, av_summed, b * NAV + n - NSLOT + 1 if not isinstance(b, int) or b else 0)
                at = 0
                for m, piece in enumerate(QK_JOBS[n]):
                    cols = pixels_of(piece)
                    o = slot[n % NSLOT][:, at * C:(at + cols) * C].rearrange("p (r c f) -> p r c f", r=piece[3], f=C)
                    ins = nc.vector.tensor_tensor(o, piece_view(qk[:, :, 0:C], piece, 0),
                                                  piece_view(qk[:, :, C:QKB], piece, 1), ALU.mult)
                    at += cols
                ins.then_inc(qk_multiplied if QK_FOLD[n] else qk_whole_ready, 1)

            def qk_fold(b, n):
                dve.wait_ge(qk_multiplied, b * NFOLD + sum(QK_FOLD[:n + 1]))
                s = slot[n % NSLOT][:, 0:sum(map(pixels_of, QK_JOBS[n])) * C].rearrange("p (x f) -> p x f", f=C)
                nc.vector.tensor_tensor(s[:, :, 0:C // 2], s[:, :, 0:C // 2], s[:, :, C // 2:C],
                                        ALU.add).then_inc(qk_folded, 1)

            def softmax_shift(b):
                for i in range(NT + 1):
                    if i < NT:
                        dve.wait_ge(gathered, b * NT + i + 1)
                        nc.vector.tensor_reduce(top[:, i].rearrange("p (w h) -> p w h", h=HEADS),
                                                prob[:, i].rearrange("p w j h -> p w h j"), AX.X,
                                                ALU.max).then_inc(maxed, 1)
                    if i >= 1:
                        dve.wait_ge(maxed, b * NT + i)
                        m = top[:, i - 1].rearrange("p (w h) -> p w h", h=HEADS)
                        nc.vector.tensor_tensor(prob[:, i - 1], prob[:, i - 1],
                                                m[:, :, None, :].to_broadcast([P, NW, NT, HEADS]),
                                                ALU.subtract).then_inc(shifted, 1)

            def softmax_divide(b):
                THIRD = NT // 3

                def third(g):
                    i = slice(g * THIRD, (g + 1) * THIRD)
                    return prob[:, i].rearrange("p i w j h -> p (i w) j h"), top[:, i].rearrange(
                        "p i (w h) -> p (i w) h", h=HEADS)

                for g in range(3):
                    e, total = third(g)
                    dve.wait_ge(exped, b * NT + (g + 1) * THIRD)
                    nc.vector.tensor_reduce(total, e.rearrange("p w j h -> p w h j"), AX.X,
                                            ALU.add).then_inc(den_summed, 1)
                for g in range(3):
                    e, total = third(g)
                    dve.wait_ge(den_summed, 3 * b + g + 1)
                    nc.vector.reciprocal(total, total).then_inc(den_inverted, 1)

            def scale_token(b, i):
                dve.wait_ge(den_inverted, 3 * b + i // (NT // 3) + 1)
                if i >= 2:
                    dve.wait_ge(av_whole_ready, b * (NAV - NAVFOLD) + i - 1)
                total = top[:, i].rearrange("p (w h) -> p w h", h=HEADS)
                for j in (slice(PJ, NT), slice(0, PJ)):
                    n = j.stop - j.start
                    dst = prob[:, i, :, j] if n < PJ else in_bank(i)
                    ins = nc.vector.tensor_tensor(dst, prob[:, i, :, j],
                                                  total[:, :, None, :].to_broadcast([P, NW, n, HEADS]), ALU.mult)
                ins.then_inc(prob_ready, 1)

            def in_bank(i):
                return bank(PROB_BANK[i % 2]).rearrange("p (w j h) -> p w j h", j=PJ, h=HEADS)

            def av_products(b, n, values):
                i, j = AV_JOBS[n]
                if n >= NSLOT:
                    dve.wait_ge(av_summed, b * NAV + n - NSLOT + 1)
                else:
                    dve.wait_ge(qk_summed, (b + 1) * NQK + n - NSLOT + 1)
                if j == 0:
                    dve.wait_ge(prob_ready, b * NT + i + 1)
                for m in range(min(2, NT - j)):
                    o = slot[n % NSLOT][:, m * NW * C:(m + 1) * NW * C]
                    ins = nc.vector.tensor_tensor(
                        o.rearrange("p (a b f) -> p a b f", a=GRID, b=GRID),
                        (in_bank(i) if j + m < PJ else prob[:, i])[:, :, j + m, None, :].to_broadcast(
                            [P, NW, HD, HEADS]),
                        window_view(values[:, :, :], *divmod(j + m, WS)), ALU.mult)
                ins.then_inc(av_multiplied if AV_FOLD[n] else av_whole_ready, 1)

            def clear_edges(b):
                dve.wait_ge(av_summed, (b + 1) * NAV)
                last = canvas.rearrange("p (r c) f -> p r c f", c=HW)
                nc.vector.memset(last[:, HW - 1, :, :], 0.0).then_inc(canvas_cleared, 1)
                nc.vector.memset(last[:, 0:HW - 1, HW - 1, :], 0.0).then_inc(canvas_cleared, 1)

            def fold_windows(b):
                dve.wait_ge(canvas_copied, (b + 1) * (NT - N_ADDS))
                dve.wait_ge(canvas_cleared, 2 * (b + 1))
                later = [k for k in range(NT) if k // WS == WS - 1 or k % WS == WS - 1]
                for n, kpos in enumerate(later):
                    if n:
                        dve.wait_ge(canvas_added, b * N_ADDS + n)
                    src = so[:, :].rearrange("p (a b c k) -> p a b c k", a=GRID, b=GRID, k=NT)[:, :, :, :, kpos]
                    dst = window_view(canvas, *divmod(kpos, WS))
                    nc.vector.tensor_tensor(dst, dst, src, ALU.add).then_inc(canvas_added, 1)

            def mlp(b, n):
                if n == 1:
                    clear_edges(b)
                if n == 2:
                    fold_windows(b)
                if BIAS_AT <= n < BIAS_AT + NHB:
                    t = n - BIAS_AT
                    w = min(BANK, PX * HID - t * BANK)
                    dve.wait_ge(hid_done, b * NHB + t + 1)
                    nc.vector.tensor_tensor(hid[:, t * BANK:t * BANK + w].rearrange("p (x f) -> p x f", f=HID),
                                            bank(6 + t % 2)[:, 0:w].rearrange("p (x f) -> p x f", f=HID),
                                            b1_mid[:, None, :].to_broadcast([P, w // HID, HID]),
                                            ALU.add).then_inc(hid_biased, 1)
                if n == SUM_AT:
                    dve.wait_ge(hid_squared, b + 1)
                    nc.vector.tensor_reduce(h_ss[:, :], hid_sq.rearrange("p (x f) -> p x f", f=HID), AX.X,
                                            ALU.add).then_inc(hid_ss, 1)
                if n == SUM_AT + 1:
                    dve.wait_ge(hid_ss, b + 1)
                    nc.vector.tensor_scalar(h_var[:, :], h_ss[:, :], 1.0 / HID, 1e-5, ALU.mult,
                                            ALU.add).then_inc(hid_var, 1)
                if n == SUM_AT + 3:
                    dve.wait_ge(hid_rstd, b + 1)
                    h3 = hid.rearrange("p (x f) -> p x f", f=HID)
                    nc.vector.tensor_tensor(h3, h3, h_rstd[:, :, None].to_broadcast([P, PX, HID]),
                                            ALU.mult).then_inc(hid_scaled, 1)
                if (n - OUT_AT) % 2 == 0 and 0 <= (n - OUT_AT) // 2 < NYB:
                    t = (n - OUT_AT) // 2
                    s, tris = t % NYSLOT, tris_in(t)
                    dve.wait_ge(y_done, b * NYB + t + 1)
                    dve.wait_ge(again_in[s], 16 * (b * y_uses(s) + t // NYSLOT + 1))
                    for half in range(0, tris, 2):
                        w = min(2, tris - half) * TRI * C
                        o = yb[s][:, half * TRI * C:half * TRI * C + w]
                        ins = nc.vector.tensor_tensor(o, o, bank(6 + half // 2)[:, 0:w], ALU.add)
                    ins.then_inc(y_added, 1)

            def block_work(b, values, preceded, follows):
                for n in range(NQK + 1):
                    if n < NQK:
                        if n == 0:
                            dve.wait_ge(proj_copied, (b + 1) * NPROJ)
                        qk_products(b, n)
                    if n >= 1 and QK_FOLD[n - 1]:
                        qk_fold(b, n - 1)
                    if preceded:
                        mlp(b - 1, n)
                    if follows and n == GN_MEAN_AT:
                        group_mean(b + 1)
                    if follows and n == GN_VAR_AT:
                        group_variance(b + 1)
                    if follows and n == GN_VAR_AT + 1:
                        group_offset(b + 1)
                if preceded:
                    for n in range(NQK + 1, MLP_STEPS):
                        mlp(b - 1, n)
                softmax_shift(b)
                softmax_divide(b)
                scale_token(b, 0)
                for n, (i, j) in enumerate(AV_JOBS):
                    av_products(b, n, values)
                    if j == 0 and i + 1 < NT:
                        scale_token(b, i + 1)

            group_mean(0)
            group_variance(0)
            group_offset(0)
            block_work(0, v[0], False, True)
            with dve.Fori(1, NBLK - 1, 2) as b:
                block_work(b, v[1], True, True)
                block_work(b + 1, v[0], True, True)
            block_work(NBLK - 1, v[1], True, False)
            for n in range(MLP_STEPS):
                mlp(NBLK - 1, n)

        @block.tensor
        def _(pe):
            def turn(src, t, to, sem_):
                for m in range(pairs_in(t)):
                    at = min((PAIRS_PER_BATCH * t + m) * 2 * C, FEAT - 2 * C)
                    ins = nc.tensor.transpose(bank(to)[:, m * P:(m + 1) * P], src[:, at:at + 2 * C],
                                              ident[:, :])
                ins.then_inc(sem_, 1)

            def project(b, k):
                kind, t, m = STEPS[k]
                if kind == "turn":
                    if t == 0:
                        pe.wait_ge(x_normed, b + 1)
                        after(pe, y_added, (b - 1) * NYB)
                    else:
                        pe.wait_ge(xt_copied, b * NXT + t)
                    turn(xb, t, TURN_BANK, xt_turned)
                    return
                pe.wait_ge(xt_copied, b * NXT + t + 1)
                if projected(k):
                    pe.wait_ge(proj_copied, b * NPROJ + projected(k))
                pairs, weights, width = (range(m, min(m + 2, pairs_in(t))), wqk, QKB) if kind == "qk" else (
                    range(pairs_in(t)), wv, C)
                for k in pairs:
                    rows, n = pair_rows(t, k), pair_pixels(t, k) * width
                    at = (k - pairs[0]) * 2 * width
                    ins = nc.tensor.matmul(bank(PROJ_BANK)[:, at:at + n], xt[t % 2][rows, k * P:(k + 1) * P],
                                           weights[rows, 2 * width - n:2 * width], start=True, stop=True)
                ins.then_inc(proj_done, 1)

            def qk_sum(b, n):
                if QK_FOLD[n]:
                    pe.wait_ge(qk_folded, b * NFOLD + sum(QK_FOLD[:n + 1]))
                else:
                    pe.wait_ge(qk_whole_ready, b * (NQK - NFOLD) + n + 1 - sum(QK_FOLD[:n + 1]))
                if n >= 4:
                    pe.wait_ge(score_copied, b * NQK + n - 3)
                elif n == ATT_BANK[0]:
                    after(pe, att_copied, b * NT)
                px = sum(map(pixels_of, QK_JOBS[n]))
                terms = HD // 2 if QK_FOLD[n] else HD
                s = slot[n % NSLOT][:, 0:px * C].rearrange("p (x d h) -> p x d h", d=HD, h=HEADS)
                for d in range(terms):
                    ins = nc.tensor.matmul(bank(n % 4)[:, 0:px * HEADS], ident[:, :], s[:, :, d, :],
                                           start=(d == 0), stop=(d == terms - 1))
                ins.then_inc(qk_summed, 1)

            def av_sum(b, n):
                i, j = AV_JOBS[n]
                if AV_FOLD[n]:
                    pe.wait_ge(av_folded, b * NAVFOLD + sum(AV_FOLD[:n + 1]))
                else:
                    pe.wait_ge(av_whole_ready, b * (NAV - NAVFOLD) + n + 1 - sum(AV_FOLD[:n + 1]))
                if j == 0:
                    if i >= 2:
                        pe.wait_ge(att_copied, b * NT + i - 1)
                    elif i == 0:
                        pe.wait_ge(score_copied, (b + 1) * NQK)
                    else:
                        after(pe, y_added, b * NYB)
                terms = 1 if AV_FOLD[n] else min(2, NT - j)
                for m in range(terms):
                    for half in range(2):
                        ins = nc.tensor.matmul(bank(ATT_BANK[i % 2] + half), ident[:, :],
                                               slot[n % NSLOT][:, m * NW * C + half * BANK:m * NW * C + (half + 1) * BANK],
                                               start=(j == 0 and m == 0), stop=(j + 2 > NT - 1 and m == terms - 1))
                ins.then_inc(av_summed, 1)

            def mlp(b, n, follows):
                if TURN_AT < n <= TURN_AT + NHB:
                    hb = n - TURN_AT - 1
                    if hb >= 2:
                        pe.wait_ge(hid_biased, b * NHB + hb - 1)
                    for s in range(2 * hb, min(2 * hb + 2, NXT)):
                        pe.wait_ge(ct_copied, b * NXT + s + 1)
                        for k in range(pairs_in(s)):
                            rows, w = pair_rows(s, k), pair_pixels(s, k) * HID
                            at = ((s % 2) * PAIRS_PER_BATCH + k) * 2 * HID
                            pad = 2 * HID if at + 4 * HID <= BANK else 0
                            ins = nc.tensor.matmul(bank(6 + hb % 2)[:, at:at + w + pad],
                                                   xt[s % 2][rows, k * P:(k + 1) * P],
                                                   w1_pair[rows, 2 * HID - w:2 * HID + pad], start=True, stop=True)
                    ins.then_inc(hid_done, 1)
                if TURN_AT <= n < TURN_AT + NHB:
                    if n == TURN_AT:
                        pe.wait_ge(canvas_added, (b + 1) * N_ADDS)
                        pe.wait_ge(proj_copied, (b + 2 if follows else b + 1) * NPROJ)
                    for t in range(2 * (n - TURN_AT), min(2 * (n - TURN_AT) + 2, NXT)):
                        if t >= 2:
                            pe.wait_ge(ct_copied, b * NXT + t - 1)
                        turn(ec, t, 4 + t % 2, ct_turned)
                if (n - TRI_AT) % 2 == 0 and 0 <= (n - TRI_AT) // 2 <= NYB:
                    t = (n - TRI_AT) // 2
                    if t == 0:
                        pe.wait_ge(hid_scaled, b + 1)
                    if t < NYB:
                        if t >= 2:
                            pe.wait_ge(gelu_done, b * NYB + t - 1)
                        for m in range(tris_in(t)):
                            at = (TRI_PER_BATCH * t + m) * TRI * HID
                            ins = nc.tensor.transpose(bank(4 + t % 2)[0:TRI * HID, m * P:(m + 1) * P],
                                                      hid[:, at:at + TRI * HID], ident[:, :])
                        ins.then_inc(ht_turned, 1)
                    if t >= 1:
                        s = t - 1
                        pe.wait_ge(gelu_done, b * NYB + s + 1)
                        if s:
                            pe.wait_ge(y_added, b * NYB + s)
                        for m in range(tris_in(s)):
                            ins = nc.tensor.matmul(bank(6 + m // 2)[:, (m % 2) * TRI * C:(m % 2 + 1) * TRI * C],
                                                   gt[s % 2][:, m * P:(m + 1) * P], w2_tri[:, :], start=True, stop=True)
                        ins.then_inc(y_done, 1)

            def block_work(b, preceded, follows):
                for n in range(NQK):
                    qk_sum(b, n)
                    if preceded:
                        mlp(b - 1, n, True)
                if preceded:
                    for n in range(NQK, MLP_STEPS):
                        mlp(b - 1, n, True)
                if follows:
                    for k in range(STEPS_SOFTMAX):
                        project(b + 1, k)
                for n in range(NAV):
                    av_sum(b, n)
                    if follows and STEPS_SOFTMAX + n < len(STEPS):
                        project(b + 1, STEPS_SOFTMAX + n)

            pe.wait_ge(ident_ready, 2)
            pe.wait_ge(weights_in, 16 * (3 * 2 + 4 * TRI + 2))
            pe.wait_ge(w1_steps, 7)
            for k in range(len(STEPS)):
                project(0, k)
            block_work(0, False, True)
            with pe.Fori(1, NBLK - 1) as b:
                block_work(b, True, True)
            block_work(NBLK - 1, True, False)
            for n in range(MLP_STEPS):
                mlp(NBLK - 1, n, False)


def kernel(x, L0_conv_w_qkv, L0_conv_pos_embedding, L0_conv_w1, L0_conv_b1, L0_conv_ln_g, L0_conv_ln_b, L0_conv_w2,
           L0_conv_b2):
    import numpy as np
    import concourse.bacc as bacc
    from concourse.bass_utils import run_bass_kernel_spmd

    HEADS, HD = 4, 16
    C = HEADS * HD
    w = np.asarray(L0_conv_w_qkv).reshape(3, HEADS, HD, C).transpose(3, 0, 2, 1).reshape(C, 3 * C)
    arrays = {
        "x": np.ascontiguousarray(x),
        "w_qk_t": np.ascontiguousarray(w[:, :2 * C]),
        "w_v_t": np.ascontiguousarray(w[:, 2 * C:]),
        "pos": np.ascontiguousarray(L0_conv_pos_embedding),
        "w1_t": np.ascontiguousarray(np.asarray(L0_conv_w1).T),
        "b1": np.ascontiguousarray(L0_conv_b1),
        "ln_g": np.ascontiguousarray(L0_conv_ln_g),
        "ln_b": np.ascontiguousarray(L0_conv_ln_b),
        "w2_t": np.ascontiguousarray(np.asarray(L0_conv_w2).T),
        "b2": np.ascontiguousarray(L0_conv_b2),
    }
    nc = bacc.Bacc("TRN2", target_bir_lowering=False, num_devices=1)
    args = [nc.dram_tensor(f"in_{n}", a.shape, mybir.dt.float32, kind="ExternalInput").ap() for n, a in arrays.items()]
    out = nc.dram_tensor("out_y", arrays["x"].shape, mybir.dt.float32, kind="ExternalOutput").ap()
    build_windowed_attention(nc, *args, out)
    r = run_bass_kernel_spmd(nc, [{f"in_{n}": a for n, a in arrays.items()}], core_ids=[0])
    return r.results[0]["out_y"]
```

```python
import concourse.bass as bass
from concourse import mybir
from contextlib import ExitStack


def build_windowed_attention(nc, x, w_qk_t, w_v_t, pos, w1_t, b1, ln_g, ln_b, w2_t, b2, out):
    fp32 = mybir.dt.float32
    ALU = mybir.AluOpType
    ACT = mybir.ActivationFunctionType
    AX = mybir.AxisListType

    HW, WS, GRID, STRIDE = 9, 3, 4, 2
    HEADS, HD = 4, 16
    C = HEADS * HD
    HID = C // 2
    PX = HW * HW
    NW = GRID * GRID
    NT = WS * WS
    NREL = (2 * WS - 1) ** 2
    P = 128
    NBLK = x.shape[0] // P
    NG = C // 2
    GN_N = 2 * PX
    FEAT = PX * C
    BANK = 512

    def places(d):
        if d == 0:
            return 0, 1, HW
        if abs(d) == 1:
            return max(0, -d), 1, HW - 1
        return max(0, -d), STRIDE, GRID

    SLOT_PX = 36
    SLOT = SLOT_PX * C
    NSLOT = 3
    pieces = []
    for dr in range(-2, 3):
        for dc in range(-2, 3):
            n_r, n_c = places(dr)[2], places(dc)[2]
            rows = min(n_r, SLOT_PX // n_c)
            pieces += [(dr, dc, r, min(rows, n_r - r)) for r in range(0, n_r, rows)]
    pixels_of = lambda piece: piece[3] * places(piece[1])[2]
    QK_JOBS = []
    for piece in sorted(pieces, key=lambda piece: (max(0, piece[0]), -pixels_of(piece))):
        for job in QK_JOBS:
            if sum(map(pixels_of, job)) + pixels_of(piece) <= SLOT_PX:
                job.append(piece)
                break
        else:
            QK_JOBS.append([piece])
    NQK = len(QK_JOBS)
    TOKENS = list(range(NT))[::-1]

    def jobs_for(i):
        return max(n for n, job in enumerate(QK_JOBS) for piece in job if piece[0] <= WS - 1 - i // WS) + 1

    NPIECES = len(pieces)
    GN_STEP = 5
    GN_PARTS = (C // 2 + GN_STEP - 1) // GN_STEP
    QK_WHOLE = (0, 1, 2, 3, 6, 9, 11, 13, 16, 18, 21, 26, 28, 31)
    QK_FOLD = [n not in QK_WHOLE for n in range(NQK)]
    NFOLD = sum(QK_FOLD)

    AV_JOBS = [(q, j) for q in range(NT) for j in range(0, NT, 2)]
    AV_PER_TOKEN = (NT + 1) // 2
    NAV = len(AV_JOBS)
    AV_FOLD = [j + 1 < NT for q, j in AV_JOBS]
    NAVFOLD = sum(AV_FOLD)
    assert NAV % 4 == 1 and NAVFOLD % 2 == 0 and not AV_FOLD[-1] and NQK % NSLOT == 0, (NAV, NQK)
    qk_slot = lambda n: (n + 1) % NSLOT

    NPAIR = (PX + 1) // 2
    PAIRS_PER_BATCH = 4
    NXT = (NPAIR + PAIRS_PER_BATCH - 1) // PAIRS_PER_BATCH
    QKB = 2 * C
    QUARTER = P // 4
    NHB = (PX * HID + BANK - 1) // BANK
    TRI = 3
    NTRI = PX // TRI
    TRI_PER_BATCH = 4
    NYB = (NTRI + TRI_PER_BATCH - 1) // TRI_PER_BATCH
    YB = TRI_PER_BATCH * TRI * C
    NYSLOT = 2

    x_v = x.rearrange("(n p) r c f -> n p (r c f)", p=P)
    out_v = out.rearrange("(n p) r c f -> n p (r c f)", p=P)

    ctx = ExitStack()
    with ctx:
        def sb(name, shape):
            return ctx.enter_context(nc.sbuf_tensor(name, shape, fp32))

        def sem(name):
            return ctx.enter_context(nc.semaphore(name))

        xb = sb("xb", [P, FEAT])
        qk = sb("qk", [P, PX, QKB])
        v = [sb(f"v{n}", [P, PX, C]) for n in range(2)]
        so = sb("so", [P, NW * NT * C])
        score = so[:, 0:PX * NREL * HEADS].rearrange("p (x e h) -> p x e h", e=NREL, h=HEADS)
        ec = sb("ec", [P, NT * NT * NW * HEADS])
        prob = ec[:, :].rearrange("p (i w j h) -> p i w j h", i=NT, w=NW, h=HEADS)
        canvas = ec[:, 0:FEAT].rearrange("p (x c) -> p x c", c=C)
        hid = ec[:, 0:PX * HID]
        hid_sq = ec[:, PX * HID:2 * PX * HID]
        slot = [sb(f"slot{n}", [P, SLOT]) for n in range(NSLOT)]
        half_slot = [half for s in slot for half in (s[:, 0:NW * C], s[:, NW * C:2 * NW * C])]
        av_kept = [half_slot[n] for n in (0, 2, 4, 5)]
        av_added = [half_slot[n] for n in (3, 1)]
        xt = [sb(f"xt{n}", [P, BANK]) for n in range(2)]
        gt = [sb(f"gt{n}", [TRI * HID + 1, BANK]) for n in range(2)]
        yb = [sb(f"yb{n}", [P, YB]) for n in range(NYSLOT)]
        top = sb("top", [P, NT, NW * HEADS])
        junk = so[:, PX * NREL * HEADS:PX * NREL * HEADS + 2 * GN_N].rearrange("p (a f) -> p a f", a=2)
        g_sum = sb("g_sum", [P, NG])
        g_neg = sb("g_neg", [P, NG])
        g_sq = sb("g_sq", [P, NG])
        g_var = sb("g_var", [P, NG])
        g_rstd = sb("g_rstd", [P, NG])
        g_off = sb("g_off", [P, NG])
        h_ss = sb("h_ss", [P, PX])
        h_var = sb("h_var", [P, PX])
        h_rstd = sb("h_rstd", [P, PX])
        minus_half = sb("minus_half", [P, PX])
        ident = sb("ident", [P, P])
        wqk = sb("wqk", [P, 2 * QKB])
        wv = sb("wv", [P, 2 * C])
        w1 = sb("w1", [P, HID])
        w1_mean = sb("w1_mean", [P, 1])
        w1_pair = sb("w1_pair", [P, 4 * HID])
        b1_row = sb("b1_row", [P, HID])
        b1_mean = sb("b1_mean", [P, 1])
        b1_mid = sb("b1_mid", [P, HID])
        b1_rest = sb("b1_rest", [P, HID])
        b1_parts = ctx.enter_context(nc.sbuf_tensor("b1_parts", [3 * QUARTER, HID], mybir.dt.bfloat16))
        b1_weights = ctx.enter_context(nc.sbuf_tensor("b1_weights", [3 * QUARTER, P], mybir.dt.bfloat16))
        w2_tri = sb("w2_tri", [TRI * HID + 1, TRI * C])
        pos_sb = sb("pos_sb", [P, NREL])
        lng = sb("lng", [TRI * HID, 1])
        lnb = sb("lnb", [TRI * HID, 1])

        ps = ctx.enter_context(nc.psum_tensor("ps", [P, 8 * BANK], fp32))

        PROB_BANK, ATT_BANK = (0, 1), (2, 6)
        TURN_BANK, PROJ_BANKS = 4, (5, 6, 7)
        PJ = BANK // (NW * HEADS)

        def bank(n, count=1):
            return ps[:, n * BANK:(n + count) * BANK]

        weights_in = sem("weights_in")
        zeroed = sem("zeroed")
        ident_ready = sem("ident_ready")
        w1_steps = sem("w1_steps")
        x_in = sem("x_in")
        again_in = [sem(f"again_in{n}") for n in range(NYSLOT)]
        y_out = [sem(f"y_out{n}") for n in range(NYSLOT)]
        gn_junk = sem("gn_junk")
        gn_sums = sem("gn_sums")
        gn_neg = sem("gn_neg")
        gn_squares = sem("gn_squares")
        gn_var = sem("gn_var")
        gn_rstd = sem("gn_rstd")
        gn_off = sem("gn_off")
        x_normed = sem("x_normed")
        xt_turned = sem("xt_turned")
        xt_copied = sem("xt_copied")
        proj_done = sem("proj_done")
        proj_copied = sem("proj_copied")
        qk_multiplied = sem("qk_multiplied")
        qk_folded = sem("qk_folded")
        qk_whole_ready = sem("qk_whole_ready")
        qk_summed = sem("qk_summed")
        score_copied = sem("score_copied")
        gathered = sem("gathered")
        maxed = sem("maxed")
        shifted = sem("shifted")
        exped = sem("exped")
        den_summed = sem("den_summed")
        den_inverted = sem("den_inverted")
        prob_ready = sem("prob_ready")
        av_multiplied = sem("av_multiplied")
        av_folded = sem("av_folded")
        av_whole_ready = sem("av_whole_ready")
        av_summed = sem("av_summed")
        att_copied = sem("att_copied")
        canvas_cleared = sem("canvas_cleared")
        canvas_copied = sem("canvas_copied")
        canvas_added = sem("canvas_added")
        ct_turned = sem("ct_turned")
        ct_copied = sem("ct_copied")
        hid_done = sem("hid_done")
        hid_copied = sem("hid_copied")
        hid_squared = sem("hid_squared")
        hid_ss = sem("hid_ss")
        hid_var = sem("hid_var")
        hid_rstd = sem("hid_rstd")
        hid_scaled = sem("hid_scaled")
        ht_turned = sem("ht_turned")
        gelu_done = sem("gelu_done")
        y_done = sem("y_done")
        y_added = sem("y_added")

        STEPS = [("turn", 0, 0)]
        for t in range(NXT):
            if t + 1 < NXT:
                STEPS.append(("turn", t + 1, 0))
            STEPS += [("qk", t, m) for m in range(0, min(PAIRS_PER_BATCH, NPAIR - PAIRS_PER_BATCH * t), 2)]
            STEPS.append(("v", t, 0))
        STEPS_SOFTMAX = 20
        step_after = {(k - STEPS_SOFTMAX) * (NAV - NSLOT) // (len(STEPS) - STEPS_SOFTMAX): k
                      for k in range(STEPS_SOFTMAX, len(STEPS))}
        projections = [k for k, step in enumerate(STEPS) if step[0] != "turn"]
        NPROJ_SOFTMAX = sum(k < STEPS_SOFTMAX for k in projections)
        NPROJ = sum((min(PAIRS_PER_BATCH, NPAIR - PAIRS_PER_BATCH * t) + 1) // 2 + 1 for t in range(NXT))
        assert NPROJ == len(projections) and len(step_after) == len(STEPS) - STEPS_SOFTMAX
        SPLIT = [STEPS_SOFTMAX * n // (NT - WS) for n in range(NT - WS + 1)]
        N_ADDS = 2 * WS - 1

        def projected(k):
            return sum(p < k for p in projections)

        def proj_bank(k):
            return PROJ_BANKS[projected(k) % 3] if k < STEPS_SOFTMAX else PROJ_BANKS[0]

        TURN_AT = [3 + t // 2 for t in range(NXT)]
        HID_AT = [TURN_AT[min(2 * k + 1, NXT - 1)] + 1 + 1 for k in range(NHB)]
        SQUARE_AT = [n + 1 for n in HID_AT]
        assert all(TURN_AT[min(NXT - 1, (PX * HID - 1) // BANK + k + 1)] <= n for k, n in enumerate(SQUARE_AT))
        SUM_AT = [n + 4 for n in SQUARE_AT]
        VAR_BANKS = (0, NHB // 2, NHB)
        VAR_AT = [SUM_AT[k - 1] + 1 for k in VAR_BANKS[1:]]
        SCALE_AT = VAR_AT[-1] + 3
        TRI_AT = [SCALE_AT + n for n in (0, 1, 2, 4, 5, 6, 8, 9)]
        OUT_AT = [n + NSLOT for n in TRI_AT[1:]]
        MLP_STEPS = max(OUT_AT) + 1
        assert len(TRI_AT) == NYB + 1
        EARLY = WS
        GATHER_AT = [23, 24, 25, 30, 31, 32]
        SHIFT_AT = [26, 27, 28]
        EXP_AT = [30, 31, 32]
        assert all(jobs_for(TOKENS[q]) <= n + 1 for q, n in enumerate(GATHER_AT))
        assert EXP_AT[0] > TRI_AT[-2] and GATHER_AT[EARLY] > TRI_AT[-2] and GATHER_AT[0] > SUM_AT[-1] + NSLOT
        assert TOKENS[EARLY - 1] * NT * NW * HEADS >= PX * HID
        GN_AT = (0, GN_PARTS + 2, 2 * GN_PARTS + 6)
        GN_MEAN_AT, GN_VAR_AT = GN_AT[1], GN_AT[2] - 1
        assert GN_AT[2] + GN_PARTS <= NQK

        def after(eng, sem_, value):
            if isinstance(value, int) and value <= 0:
                return
            eng.wait_ge(sem_, value)

        def hid_bank(t):
            return slice(t * BANK, min((t + 1) * BANK, PX * HID))

        def var_pixels(k):
            return slice(VAR_BANKS[k] * BANK // HID, min(VAR_BANKS[k + 1] * BANK // HID, PX))

        def y_uses(s):
            return len(range(s, NYB, NYSLOT))

        def pair_rows(t, m):
            return slice(C, 2 * C) if PAIRS_PER_BATCH * t + m == NPAIR - 1 else slice(0, 2 * C)

        def pair_pixels(t, m):
            return 1 if PAIRS_PER_BATCH * t + m == NPAIR - 1 else 2

        def pairs_in(t):
            return min(PAIRS_PER_BATCH, NPAIR - PAIRS_PER_BATCH * t)

        def tris_in(t):
            return min(TRI_PER_BATCH, NTRI - TRI_PER_BATCH * t)

        def window_view(buf, ki, kj):
            g = buf.rearrange("p (r c) f -> p r c f", c=HW)
            return g[:, ki:ki + STRIDE * (GRID - 1) + 1:STRIDE, kj:kj + STRIDE * (GRID - 1) + 1:STRIDE, :]

        def scores_of(i):
            ki, kj = divmod(i, WS)
            s = score.rearrange("p (r c) (a b) h -> p r c a b h", c=HW, b=2 * WS - 1)
            s = s[:, ki:ki + STRIDE * (GRID - 1) + 1:STRIDE, kj:kj + STRIDE * (GRID - 1) + 1:STRIDE]
            return s[:, :, :, WS - 1 - ki:2 * WS - 1 - ki, WS - 1 - kj:2 * WS - 1 - kj, :]

        def piece_view(buf, piece, shifted_by):
            dr, dc, r, n = piece
            (r0, rs, _), (c0, cs, nc_) = places(dr), places(dc)
            r0, c0 = r0 + rs * r + dr * shifted_by, c0 + dc * shifted_by
            g = buf.rearrange("p (r c) f -> p r c f", c=HW)
            return g[:, r0:r0 + rs * (n - 1) + 1:rs, c0:c0 + cs * (nc_ - 1) + 1:cs, :]

        block = ctx.enter_context(nc.Block())

        @block.sync
        def _(sp):
            def load_x(b):
                sp.wait_ge(xt_turned, b * NXT)
                sp.dma_start(xb[:, :], x_v[b]).then_inc(x_in, 16)

            sp.dma_start(xb[:, :], x_v[0]).then_inc(x_in, 16)
            for m in range(2):
                sp.wait_ge(zeroed, 4)
                rows = slice(m * C, (m + 1) * C)
                sp.dma_start(wqk[rows, m * QKB:(m + 1) * QKB], w_qk_t).then_inc(weights_in, 16)
                sp.dma_start(wv[rows, m * C:(m + 1) * C], w_v_t).then_inc(weights_in, 16)
                sp.dma_start(w1[rows, :], w1_t).then_inc(weights_in, 16)
            for m in range(TRI):
                rows = slice(m * HID, (m + 1) * HID)
                sp.dma_start(w2_tri[rows, m * C:(m + 1) * C], w2_t).then_inc(weights_in, 16)
                sp.dma_start(w2_tri[TRI * HID:TRI * HID + 1, m * C:(m + 1) * C],
                             b2.rearrange("(a n) -> a n", a=1)).then_inc(weights_in, 16)
                sp.dma_start(lng[rows, :], ln_g.rearrange("(n a) -> n a", a=1)).then_inc(weights_in, 16)
                sp.dma_start(lnb[rows, :], ln_b.rearrange("(n a) -> n a", a=1)).then_inc(weights_in, 16)
            sp.dma_start(b1_row[:, :], b1.partition_broadcast(P)).then_inc(weights_in, 16)
            sp.dma_start(pos_sb[:, :], pos.rearrange("a b -> (a b)").partition_broadcast(P)).then_inc(weights_in, 16)

            def block_io(b, follows):
                if follows:
                    load_x(b + 2)
                for t in range(NYB):
                    s, n = t % NYSLOT, tris_in(t) * TRI * C
                    after(sp, y_out[s], 16 * (b * y_uses(s) + t // NYSLOT))
                    sp.dma_start(yb[s][:, 0:n], x_v[b][:, t * YB:t * YB + n]).then_inc(again_in[s], 16)
                    if t >= 1:
                        store(b, t - 1)
                store(b, NYB - 1)

            def store(b, t):
                s, n = t % NYSLOT, tris_in(t) * TRI * C
                sp.wait_ge(y_added, b * NYB + t + 1)
                sp.dma_start(out_v[b][:, t * YB:t * YB + n], yb[s][:, 0:n]).then_inc(y_out[s], 16)

            load_x(1)
            block_io(0, True)
            with sp.Fori(1, NBLK - 2) as b:
                block_io(b, True)
            block_io(NBLK - 2, False)
            block_io(NBLK - 1, False)
            for s in range(NYSLOT):
                sp.wait_ge(y_out[s], 16 * NBLK * y_uses(s))

        @block.gpsimd
        def _(pool):
            nc.gpsimd.memset(wqk[:, :], 0.0).then_inc(zeroed, 1)
            nc.gpsimd.memset(wv[:, :], 0.0).then_inc(zeroed, 1)
            nc.gpsimd.memset(w1_pair[:, :], 0.0).then_inc(zeroed, 1)
            nc.gpsimd.memset(w2_tri[:, :], 0.0).then_inc(zeroed, 1)
            nc.gpsimd.memset(ident[:, :], 0.0).then_inc(ident_ready, 1)
            nc.gpsimd.memset(minus_half[:, :], -0.5).then_inc(zeroed, 1)
            pool.wait_ge(ident_ready, 1)
            nc.gpsimd.affine_select(out=ident[:, :], in_=ident[:, :], compare_op=ALU.not_equal, fill=1.0,
                                    base=0, pattern=[[-1, P]], channel_multiplier=1).then_inc(ident_ready, 1)

            def group_rstd(b):
                pool.wait_ge(gn_var, b + 1)
                nc.gpsimd.tensor_tensor(g_rstd[:, :], g_var[:, :], minus_half[:, 0:NG], ALU.pow).then_inc(gn_rstd, 1)

            def pixel_rstd(b, k):
                pool.wait_ge(hid_var, 2 * b + k + 1)
                nc.gpsimd.tensor_tensor(h_rstd[:, var_pixels(k)], h_var[:, var_pixels(k)],
                                        minus_half[:, var_pixels(k)], ALU.pow).then_inc(hid_rstd, 1)

            def add_pairs(b):
                for n in range(NAV):
                    if AV_FOLD[n]:
                        pool.wait_ge(av_multiplied, b * NAVFOLD + sum(AV_FOLD[:n + 1]))
                        kept, added = av_kept[n % 4], av_added[sum(AV_FOLD[:n]) % 2]
                        nc.gpsimd.tensor_tensor(kept, kept, added, ALU.add).then_inc(av_folded, 1)

            def block_work(b, preceded, follows):
                if preceded:
                    pixel_rstd(b - 1, 0)
                    pixel_rstd(b - 1, 1)
                if follows:
                    group_rstd(b + 1)
                add_pairs(b)

            pool.wait_ge(zeroed, 5)
            group_rstd(0)
            block_work(0, False, True)
            with pool.Fori(1, NBLK - 1) as b:
                block_work(b, True, True)
            block_work(NBLK - 1, True, False)
            pixel_rstd(NBLK - 1, 0)
            pixel_rstd(NBLK - 1, 1)

        @block.scalar
        def _(act):
            xg = xb[:, :].rearrange("p (x g c) -> p g x c", g=NG, c=2)

            def group_norm(b, part):
                first = part % GN_PARTS * GN_STEP
                groups = range(first, min(NG, first + GN_STEP))
                if part < GN_PARTS:
                    if part == 0:
                        act.wait_ge(x_in, 16 * (b + 1))
                    for g in groups:
                        nc.scalar.activation(xg[:, g], xg[:, g], ACT.Copy,
                                             accum_out=g_sum[:, g:g + 1]).then_inc(gn_junk, 1)
                elif part < 2 * GN_PARTS:
                    if part == GN_PARTS:
                        act.wait_ge(gn_neg, b + 1)
                    for g in groups:
                        after(act, gn_junk, (2 * b + 1) * NG + g - 1)
                        nc.scalar.activation(junk[:, g % 2].rearrange("p (x c) -> p x c", c=2), xg[:, g], ACT.Square,
                                             bias=g_neg[:, g:g + 1], accum_out=g_sq[:, g:g + 1]).then_inc(gn_junk, 1)
                else:
                    if part == 2 * GN_PARTS:
                        act.wait_ge(gn_off, b + 1)
                    for g in groups:
                        ins = nc.scalar.activation(xg[:, g], xg[:, g], ACT.Identity, bias=g_off[:, g:g + 1],
                                                   scale=g_rstd[:, g:g + 1])
                    if part == 3 * GN_PARTS - 1:
                        ins.then_inc(x_normed, 1)

            def project(b, parity, k):
                kind, t, m = STEPS[k]
                if kind == "turn":
                    act.wait_ge(xt_turned, b * NXT + t + 1)
                    if t >= 2:
                        act.wait_ge(proj_done, b * NPROJ + projected(STEPS.index(("v", t - 2, 0)) + 1))
                    else:
                        after(act, hid_done, (b - 1) * NHB)
                    nc.scalar.activation(xt[t % 2][:, 0:pairs_in(t) * P], bank(TURN_BANK)[:, 0:pairs_in(t) * P],
                                         ACT.Copy).then_inc(xt_copied, 1)
                    return
                act.wait_ge(proj_done, b * NPROJ + projected(k + 1))
                if kind == "qk":
                    px = 2 * (PAIRS_PER_BATCH * t + m)
                    n, width, dst = min(4, PX - px), QKB, qk
                else:
                    px = 2 * PAIRS_PER_BATCH * t
                    n, width, dst = min(8, PX - px), C, v[parity]
                nc.scalar.activation(dst[:, px:px + n, :],
                                     bank(proj_bank(k))[:, 0:n * width].rearrange("p (x f) -> p x f", f=width),
                                     ACT.Copy).then_inc(proj_copied, 1)

            def copy_scores(b, n):
                if n == 0:
                    after(act, canvas_added, b * N_ADDS)
                act.wait_ge(qk_summed, b * NQK + n + 1)
                at = 0
                for piece in QK_JOBS[n]:
                    dr, dc, _, rows = piece
                    e = (dr + WS - 1) * (2 * WS - 1) + dc + WS - 1
                    cols = pixels_of(piece)
                    ins = nc.scalar.activation(
                        piece_view(score[:, :, e, :], piece, 0),
                        bank(n % 4)[:, at * HEADS:(at + cols) * HEADS].rearrange("p (r c h) -> p r c h", r=rows, h=HEADS),
                        ACT.Identity, bias=pos_sb[:, e:e + 1], scale=HD ** -0.5)
                    at += cols
                ins.then_inc(score_copied, 1)

            def mlp(b, n, follows):
                if n in HID_AT:
                    t = HID_AT.index(n)
                    at = hid_bank(t)
                    act.wait_ge(hid_done, b * NHB + t + 1)
                    nc.scalar.activation(hid[:, at], bank(6 + t % 2)[:, 0:at.stop - at.start],
                                         ACT.Copy).then_inc(hid_copied, 1)
                for t in range(NXT):
                    if TURN_AT[t] == n:
                        act.wait_ge(ct_turned, b * NXT + t + 1)
                        if t < 2:
                            act.wait_ge(proj_done, (b + 2 if follows else b + 1) * NPROJ)
                        else:
                            act.wait_ge(hid_done, b * NHB + (t - 2) // 2 + 1)
                        nc.scalar.activation(xt[t % 2][:, 0:pairs_in(t) * P], bank(4 + t % 2)[:, 0:pairs_in(t) * P],
                                             ACT.Copy).then_inc(ct_copied, 1)
                if n in SQUARE_AT:
                    t = SQUARE_AT.index(n)
                    act.wait_ge(hid_copied, b * NHB + t + 1)
                    nc.scalar.activation(hid_sq[:, hid_bank(t)], hid[:, hid_bank(t)],
                                         ACT.Square).then_inc(hid_squared, 1)
                if n in TRI_AT[:NYB]:
                    t = TRI_AT.index(n)
                    w = tris_in(t) * P
                    act.wait_ge(ht_turned, b * NYB + t + 1)
                    if t >= 2:
                        act.wait_ge(y_done, b * NYB + t - 1)
                    nc.scalar.activation(gt[t % 2][0:TRI * HID, 0:w], bank(4 + t % 2)[0:TRI * HID, 0:w], ACT.Gelu,
                                         bias=lnb[:, :], scale=lng[:, :]).then_inc(gelu_done, 1)

            def gather(b, q):
                i = TOKENS[q]
                act.wait_ge(score_copied, b * NQK + jobs_for(i))
                if q < EARLY:
                    after(act, hid_ss, b * NHB)
                else:
                    after(act, ht_turned, b * NYB)
                for k in range(WS):
                    ins = nc.scalar.activation(
                        prob[:, i].rearrange("p (a b) (k f) h -> p a b k (f h)", a=GRID, k=WS)[:, :, :, k],
                        scores_of(i)[:, :, :, k].rearrange("p a b f h -> p a b (f h)"), ACT.Copy)
                ins.then_inc(gathered, 1)

            def exponentials(b, q):
                act.wait_ge(shifted, b * NT + q + 1)
                nc.scalar.activation(prob[:, TOKENS[q]], prob[:, TOKENS[q]], ACT.Exp).then_inc(exped, 1)

            def block_work(b, parity, preceded, follows):
                for n in range(NQK):
                    copy_scores(b, n)
                    if preceded:
                        mlp(b - 1, n, True)
                    for p, start in enumerate(GN_AT):
                        if follows and start <= n < start + GN_PARTS:
                            group_norm(b + 1, p * GN_PARTS + n - start)
                    if n in GATHER_AT:
                        gather(b, GATHER_AT.index(n))
                    if n in EXP_AT:
                        exponentials(b, EXP_AT.index(n))
                for q in range(len(GATHER_AT), NT):
                    gather(b, q)
                for q in range(EARLY, NT):
                    exponentials(b, q)
                    if follows:
                        for k in range(SPLIT[q - EARLY], SPLIT[q - EARLY + 1]):
                            project(b + 1, 1 - parity, k)
                for n, (q, j) in enumerate(AV_JOBS):
                    if follows and n in step_after:
                        project(b + 1, 1 - parity, step_after[n])
                    if (n + 1) % AV_PER_TOKEN:
                        continue
                    act.wait_ge(av_summed, b * NAV + n + 1)
                    o = so[:, :].rearrange("p (w i h d) -> p w i h d", w=NW, i=NT, h=HEADS)[:, :, TOKENS[q]]
                    s = bank(ATT_BANK[q % 2], 2).rearrange("p (w d h) -> p w h d", w=NW, h=HEADS)
                    for half in range(2):
                        w = slice(half * (NW // 2), (half + 1) * (NW // 2))
                        ins = nc.scalar.activation(o[:, w], s[:, w], ACT.Copy)
                    ins.then_inc(att_copied, 1)
                act.wait_ge(att_copied, (b + 1) * NT)
                for ki in range(WS - 1):
                    for kj in range(WS - 1):
                        nc.scalar.activation(window_view(canvas, ki, kj), folded(ki * WS + kj),
                                             ACT.Copy).then_inc(canvas_copied, 1)

            def folded(kpos):
                return so[:, :].rearrange("p (a b c k) -> p a b c k", a=GRID, b=GRID, k=NT)[:, :, :, :, kpos]

            act.wait_ge(weights_in, 16 * (3 * 2 + 4 * TRI + 2))
            act.wait_ge(zeroed, 5)
            for part in range(3 * GN_PARTS):
                group_norm(0, part)
            for k in range(len(STEPS)):
                project(0, 0, k)
            block_work(0, 0, False, True)
            with act.Fori(1, NBLK - 1, 2) as b:
                block_work(b, 1, True, True)
                block_work(b + 1, 0, True, True)
            block_work(NBLK - 1, 1, True, False)
            for n in range(MLP_STEPS):
                mlp(NBLK - 1, n, False)

        @block.vector
        def _(dve):
            dve.wait_ge(weights_in, 16 * (3 * 2 + 4 * TRI + 2))
            dve.wait_ge(zeroed, 5)
            for n in range(2):
                nc.vector.memset(gt[n][TRI * HID:TRI * HID + 1, :], 1.0)
            nc.vector.tensor_reduce(w1_mean[:, :], w1[:, :], AX.X, ALU.add).then_inc(w1_steps, 1)
            nc.vector.tensor_reduce(b1_mean[:, :], b1_row[:, :], AX.X, ALU.add).then_inc(w1_steps, 1)
            dve.wait_ge(w1_steps, 2)
            nc.vector.tensor_scalar(w1_mean[:, :], w1_mean[:, :], 1.0 / HID, None, ALU.mult).then_inc(w1_steps, 1)
            nc.vector.tensor_scalar(b1_mean[:, :], b1_mean[:, :], 1.0 / HID, None, ALU.mult).then_inc(w1_steps, 1)
            dve.wait_ge(w1_steps, 4)
            for m in range(2):
                rows = slice(m * C, (m + 1) * C)
                nc.vector.tensor_scalar(w1_pair[rows, m * HID:(m + 1) * HID], w1[rows, :], w1_mean[rows, :], None,
                                        ALU.subtract).then_inc(w1_steps, 1)
            nc.vector.tensor_scalar(b1_mid[:, :], b1_row[:, :], b1_mean[:, :], None, ALU.subtract).then_inc(w1_steps, 1)
            nc.vector.memset(b1_weights[:, :], 1.0 / QUARTER).then_inc(w1_steps, 1)
            for k in range(3):
                rows = slice(k * QUARTER, (k + 1) * QUARTER)
                for m in range(k + 1):
                    rest = b1_mid if m == 0 else b1_rest
                    dve.wait_ge(w1_steps, 8 + k * (k + 1) + 2 * m)
                    nc.vector.tensor_copy(b1_parts[rows, :], rest[rows, :]).then_inc(w1_steps, 1)
                    dve.wait_ge(w1_steps, 9 + k * (k + 1) + 2 * m)
                    nc.vector.tensor_tensor(b1_rest[rows, :], rest[rows, :], b1_parts[rows, :],
                                            ALU.subtract).then_inc(w1_steps, 1)

            def group_mean(b):
                dve.wait_ge(gn_junk, (2 * b + 1) * NG)
                nc.vector.tensor_scalar(g_neg[:, :], g_sum[:, :], -1.0 / GN_N, None, ALU.mult).then_inc(gn_neg, 1)

            def group_variance(b):
                dve.wait_ge(gn_junk, (2 * b + 2) * NG)
                nc.vector.tensor_scalar(g_var[:, :], g_sq[:, :], 1.0 / GN_N, 1e-5, ALU.mult, ALU.add).then_inc(gn_var, 1)

            def group_offset(b):
                dve.wait_ge(gn_rstd, b + 1)
                nc.vector.tensor_tensor(g_off[:, :], g_neg[:, :], g_rstd[:, :], ALU.mult).then_inc(gn_off, 1)

            def qk_products(b, n):
                if n >= NSLOT:
                    dve.wait_ge(qk_summed, b * NQK + n - NSLOT + 1)
                else:
                    after(dve, av_summed, b * NAV - (3, 1, 0)[n] if not isinstance(b, int) or b else 0)
                    if n == 0:
                        after(dve, av_folded, b * NAVFOLD - 1 if not isinstance(b, int) or b else 0)
                at = 0
                for m, piece in enumerate(QK_JOBS[n]):
                    cols = pixels_of(piece)
                    o = slot[qk_slot(n)][:, at * C:(at + cols) * C].rearrange("p (r c f) -> p r c f", r=piece[3], f=C)
                    ins = nc.vector.tensor_tensor(o, piece_view(qk[:, :, 0:C], piece, 0),
                                                  piece_view(qk[:, :, C:QKB], piece, 1), ALU.mult)
                    at += cols
                ins.then_inc(qk_multiplied if QK_FOLD[n] else qk_whole_ready, 1)

            def qk_fold(b, n):
                dve.wait_ge(qk_multiplied, b * NFOLD + sum(QK_FOLD[:n + 1]))
                s = slot[qk_slot(n)][:, 0:sum(map(pixels_of, QK_JOBS[n])) * C].rearrange("p (x f) -> p x f", f=C)
                nc.vector.tensor_tensor(s[:, :, 0:C // 2], s[:, :, 0:C // 2], s[:, :, C // 2:C],
                                        ALU.add).then_inc(qk_folded, 1)

            def find_max(b, q):
                i = TOKENS[q]
                dve.wait_ge(gathered, b * NT + q + 1)
                nc.vector.tensor_reduce(top[:, i].rearrange("p (w h) -> p w h", h=HEADS),
                                        prob[:, i].rearrange("p w j h -> p w h j"), AX.X, ALU.max).then_inc(maxed, 1)

            def take_max_away(b, q):
                i = TOKENS[q]
                dve.wait_ge(maxed, b * NT + q + 1)
                m = top[:, i].rearrange("p (w h) -> p w h", h=HEADS)
                nc.vector.tensor_tensor(prob[:, i], prob[:, i], m[:, :, None, :].to_broadcast([P, NW, NT, HEADS]),
                                        ALU.subtract).then_inc(shifted, 1)

            def totals(b, g):
                third = NT // 3
                i = slice(NT - (g + 1) * third, NT - g * third)
                e = prob[:, i].rearrange("p i w j h -> p (i w) h j")
                total = top[:, i].rearrange("p i (w h) -> p (i w) h", h=HEADS)
                dve.wait_ge(exped, b * NT + (g + 1) * third)
                nc.vector.tensor_reduce(total, e, AX.X, ALU.add).then_inc(den_summed, 1)
                dve.wait_ge(den_summed, 3 * b + g + 1)
                nc.vector.reciprocal(total, total).then_inc(den_inverted, 1)

            def scale_token(b, q):
                i = TOKENS[q]
                dve.wait_ge(den_inverted, 3 * b + q // (NT // 3) + 1)
                if q >= 2:
                    dve.wait_ge(av_whole_ready, b * (NAV - NAVFOLD) + q - 1)
                total = top[:, i].rearrange("p (w h) -> p w h", h=HEADS)
                for j in (slice(PJ, NT), slice(0, PJ)):
                    n = j.stop - j.start
                    dst = prob[:, i, :, j] if n < PJ else in_bank(q)
                    ins = nc.vector.tensor_tensor(dst, prob[:, i, :, j],
                                                  total[:, :, None, :].to_broadcast([P, NW, n, HEADS]), ALU.mult)
                ins.then_inc(prob_ready, 1)

            def in_bank(q):
                return bank(PROB_BANK[q % 2]).rearrange("p (w j h) -> p w j h", j=PJ, h=HEADS)

            def av_products(b, n, values):
                q, j = AV_JOBS[n]
                i = TOKENS[q]
                f = sum(AV_FOLD[:n])
                if n >= 4:
                    dve.wait_ge(av_summed, b * NAV + n - 3)
                elif n == 0:
                    dve.wait_ge(qk_summed, (b + 1) * NQK)
                if j == 0:
                    dve.wait_ge(prob_ready, b * NT + q + 1)
                for m in range(min(2, NT - j)):
                    if m and f >= 2:
                        dve.wait_ge(av_folded, b * NAVFOLD + f - 1)
                    o = av_added[f % 2] if m else av_kept[n % 4]
                    ins = nc.vector.tensor_tensor(
                        o.rearrange("p (a b f) -> p a b f", a=GRID, b=GRID),
                        (in_bank(q) if j + m < PJ else prob[:, i])[:, :, j + m, None, :].to_broadcast(
                            [P, NW, HD, HEADS]),
                        window_view(values[:, :, :], *divmod(j + m, WS)), ALU.mult)
                ins.then_inc(av_multiplied if AV_FOLD[n] else av_whole_ready, 1)

            def clear_edges(b):
                dve.wait_ge(av_summed, (b + 1) * NAV)
                last = canvas.rearrange("p (r c) f -> p r c f", c=HW)
                nc.vector.memset(last[:, HW - 1, :, :], 0.0).then_inc(canvas_cleared, 1)
                nc.vector.memset(last[:, 0:HW - 1, HW - 1, :], 0.0).then_inc(canvas_cleared, 1)

            def fold_windows(b):
                dve.wait_ge(canvas_copied, (b + 1) * (NT - N_ADDS))
                dve.wait_ge(canvas_cleared, 2 * (b + 1))
                later = [k for k in range(NT) if k // WS == WS - 1 or k % WS == WS - 1]
                for n, kpos in enumerate(later):
                    if n:
                        dve.wait_ge(canvas_added, b * N_ADDS + n)
                    src = so[:, :].rearrange("p (a b c k) -> p a b c k", a=GRID, b=GRID, k=NT)[:, :, :, :, kpos]
                    dst = window_view(canvas, *divmod(kpos, WS))
                    nc.vector.tensor_tensor(dst, dst, src, ALU.add).then_inc(canvas_added, 1)

            def mlp(b, n):
                if n == 1:
                    clear_edges(b)
                if n == 2:
                    fold_windows(b)
                if n in SUM_AT:
                    t = SUM_AT.index(n)
                    squares = hid_sq[:, hid_bank(t)].rearrange("p (x f) -> p x f", f=HID)
                    x0 = t * BANK // HID
                    dve.wait_ge(hid_squared, b * NHB + t + 1)
                    nc.vector.tensor_reduce(h_ss[:, x0:x0 + squares.shape[1]], squares, AX.X,
                                            ALU.add).then_inc(hid_ss, 1)
                if n in VAR_AT:
                    k = VAR_AT.index(n)
                    dve.wait_ge(hid_ss, b * NHB + VAR_BANKS[k + 1])
                    nc.vector.tensor_scalar(h_var[:, var_pixels(k)], h_ss[:, var_pixels(k)], 1.0 / HID, 1e-5,
                                            ALU.mult, ALU.add).then_inc(hid_var, 1)
                if n == SCALE_AT:
                    dve.wait_ge(hid_rstd, 2 * (b + 1))
                    dve.wait_ge(hid_copied, (b + 1) * NHB)
                    h3 = hid.rearrange("p (x f) -> p x f", f=HID)
                    nc.vector.tensor_tensor(h3, h3, h_rstd[:, :, None].to_broadcast([P, PX, HID]),
                                            ALU.mult).then_inc(hid_scaled, 1)
                if n in OUT_AT:
                    t = OUT_AT.index(n)
                    s, tris = t % NYSLOT, tris_in(t)
                    dve.wait_ge(y_done, b * NYB + t + 1)
                    dve.wait_ge(again_in[s], 16 * (b * y_uses(s) + t // NYSLOT + 1))
                    for half in range(0, tris, 2):
                        w = min(2, tris - half) * TRI * C
                        o = yb[s][:, half * TRI * C:half * TRI * C + w]
                        ins = nc.vector.tensor_tensor(o, o, bank(6 + half // 2)[:, 0:w], ALU.add)
                    ins.then_inc(y_added, 1)

            def block_work(b, values, preceded, follows):
                for n in range(NQK + 1):
                    if n < NQK:
                        if n == 0:
                            dve.wait_ge(proj_copied, (b + 1) * NPROJ)
                        qk_products(b, n)
                    if n >= 1 and QK_FOLD[n - 1]:
                        qk_fold(b, n - 1)
                    if preceded:
                        mlp(b - 1, n)
                    if n in SHIFT_AT:
                        find_max(b, SHIFT_AT.index(n))
                    if n - 1 in SHIFT_AT:
                        take_max_away(b, SHIFT_AT.index(n - 1))
                    if follows and n == GN_MEAN_AT:
                        group_mean(b + 1)
                    if follows and n == GN_VAR_AT:
                        group_variance(b + 1)
                    if follows and n == GN_VAR_AT + 3:
                        group_offset(b + 1)
                if preceded:
                    for n in range(NQK + 1, MLP_STEPS):
                        mlp(b - 1, n)
                for q in range(EARLY, NT + 1):
                    if q < NT:
                        find_max(b, q)
                    if q > EARLY:
                        take_max_away(b, q - 1)
                    if q == 2 * EARLY:
                        totals(b, 0)
                scale_token(b, 0)
                for n, (q, j) in enumerate(AV_JOBS):
                    av_products(b, n, values)
                    if j == 0 and q + 1 < NT:
                        scale_token(b, q + 1)
                    if j == 4 and q in (0, 1):
                        totals(b, q + 1)

            group_mean(0)
            group_variance(0)
            group_offset(0)
            block_work(0, v[0], False, True)
            with dve.Fori(1, NBLK - 1, 2) as b:
                block_work(b, v[1], True, True)
                block_work(b + 1, v[0], True, True)
            block_work(NBLK - 1, v[1], True, False)
            for n in range(MLP_STEPS):
                mlp(NBLK - 1, n)

        @block.tensor
        def _(pe):
            def turn(src, t, to, sem_):
                for m in range(pairs_in(t)):
                    at = min((PAIRS_PER_BATCH * t + m) * 2 * C, FEAT - 2 * C)
                    ins = nc.tensor.transpose(bank(to)[:, m * P:(m + 1) * P], src[:, at:at + 2 * C],
                                              ident[:, :])
                ins.then_inc(sem_, 1)

            def project(b, k):
                kind, t, m = STEPS[k]
                if kind == "turn":
                    if t == 0:
                        pe.wait_ge(x_normed, b + 1)
                        after(pe, y_added, (b - 1) * NYB)
                    else:
                        pe.wait_ge(xt_copied, b * NXT + t)
                    turn(xb, t, TURN_BANK, xt_turned)
                    return
                pe.wait_ge(xt_copied, b * NXT + t + 1)
                before = projected(k) - 2 if k < STEPS_SOFTMAX else projected(k)
                if before > 0:
                    pe.wait_ge(proj_copied, b * NPROJ + before)
                to = proj_bank(k)
                pairs, weights, width = (range(m, min(m + 2, pairs_in(t))), wqk, QKB) if kind == "qk" else (
                    range(pairs_in(t)), wv, C)
                for k in pairs:
                    rows, n = pair_rows(t, k), pair_pixels(t, k) * width
                    at = (k - pairs[0]) * 2 * width
                    ins = nc.tensor.matmul(bank(to)[:, at:at + n], xt[t % 2][rows, k * P:(k + 1) * P],
                                           weights[rows, 2 * width - n:2 * width], start=True, stop=True)
                ins.then_inc(proj_done, 1)

            def qk_sum(b, n):
                if QK_FOLD[n]:
                    pe.wait_ge(qk_folded, b * NFOLD + sum(QK_FOLD[:n + 1]))
                else:
                    pe.wait_ge(qk_whole_ready, b * (NQK - NFOLD) + n + 1 - sum(QK_FOLD[:n + 1]))
                if n >= 4:
                    pe.wait_ge(score_copied, b * NQK + n - 3)
                elif n == ATT_BANK[0]:
                    after(pe, att_copied, b * NT)
                px = sum(map(pixels_of, QK_JOBS[n]))
                terms = HD // 2 if QK_FOLD[n] else HD
                s = slot[qk_slot(n)][:, 0:px * C].rearrange("p (x d h) -> p x d h", d=HD, h=HEADS)
                for d in range(terms):
                    ins = nc.tensor.matmul(bank(n % 4)[:, 0:px * HEADS], ident[:, :], s[:, :, d, :],
                                           start=(d == 0), stop=(d == terms - 1))
                ins.then_inc(qk_summed, 1)

            def av_sum(b, n, follows):
                q, j = AV_JOBS[n]
                if AV_FOLD[n]:
                    pe.wait_ge(av_folded, b * NAVFOLD + sum(AV_FOLD[:n + 1]))
                else:
                    pe.wait_ge(av_whole_ready, b * (NAV - NAVFOLD) + n + 1 - sum(AV_FOLD[:n + 1]))
                if j == 0:
                    if q >= 2:
                        pe.wait_ge(att_copied, b * NT + q - 1)
                    elif q == 0:
                        pe.wait_ge(score_copied, (b + 1) * NQK)
                    else:
                        after(pe, y_added, b * NYB)
                        if follows:
                            pe.wait_ge(proj_copied, (b + 1) * NPROJ + NPROJ_SOFTMAX)
                for half in range(2):
                    ins = nc.tensor.matmul(bank(ATT_BANK[q % 2] + half), ident[:, :],
                                           av_kept[n % 4][:, half * BANK:(half + 1) * BANK],
                                           start=(j == 0), stop=(j + 2 > NT - 1))
                ins.then_inc(av_summed, 1)

            def mlp(b, n, follows):
                for t in range(NXT):
                    if TURN_AT[t] + 1 != n:
                        continue
                    hb = t // 2
                    if t % 2 == 0:
                        if hb >= 2:
                            pe.wait_ge(hid_copied, b * NHB + hb - 1)
                        nc.tensor.matmul(bank(6 + hb % 2), b1_weights[:, :],
                                         b1_parts[:, None, :].to_broadcast([3 * QUARTER, BANK // HID, HID]),
                                         start=True, stop=False)
                    pe.wait_ge(ct_copied, b * NXT + t + 1)
                    for k in range(pairs_in(t)):
                        rows, w = pair_rows(t, k), pair_pixels(t, k) * HID
                        at = ((t % 2) * PAIRS_PER_BATCH + k) * 2 * HID
                        pad = 2 * HID if at + 4 * HID <= BANK else 0
                        ins = nc.tensor.matmul(bank(6 + hb % 2)[:, at:at + w + pad], xt[t % 2][rows, k * P:(k + 1) * P],
                                               w1_pair[rows, 2 * HID - w:2 * HID + pad], start=False,
                                               stop=k == pairs_in(t) - 1 and (t % 2 == 1 or t == NXT - 1))
                    if t % 2 or t == NXT - 1:
                        ins.then_inc(hid_done, 1)
                for t in range(NXT):
                    if TURN_AT[t] != n:
                        continue
                    if t == 0:
                        pe.wait_ge(canvas_added, (b + 1) * N_ADDS)
                        pe.wait_ge(proj_copied, (b + 2 if follows else b + 1) * NPROJ)
                    elif t >= 2:
                        pe.wait_ge(ct_copied, b * NXT + t - 1)
                    turn(ec, t, 4 + t % 2, ct_turned)
                if n in TRI_AT:
                    t = TRI_AT.index(n)
                    if t == 0:
                        pe.wait_ge(hid_scaled, b + 1)
                    if t < NYB:
                        if t >= 2:
                            pe.wait_ge(gelu_done, b * NYB + t - 1)
                        for m in range(tris_in(t)):
                            at = (TRI_PER_BATCH * t + m) * TRI * HID
                            ins = nc.tensor.transpose(bank(4 + t % 2)[0:TRI * HID, m * P:(m + 1) * P],
                                                      hid[:, at:at + TRI * HID], ident[:, :])
                        ins.then_inc(ht_turned, 1)
                    if t >= 1:
                        s = t - 1
                        pe.wait_ge(gelu_done, b * NYB + s + 1)
                        if s:
                            pe.wait_ge(y_added, b * NYB + s)
                        for m in range(tris_in(s)):
                            ins = nc.tensor.matmul(bank(6 + m // 2)[:, (m % 2) * TRI * C:(m % 2 + 1) * TRI * C],
                                                   gt[s % 2][:, m * P:(m + 1) * P], w2_tri[:, :], start=True, stop=True)
                        ins.then_inc(y_done, 1)

            def block_work(b, preceded, follows):
                for n in range(NQK):
                    qk_sum(b, n)
                    if preceded:
                        mlp(b - 1, n, True)
                if preceded:
                    for n in range(NQK, MLP_STEPS):
                        mlp(b - 1, n, True)
                if follows:
                    for k in range(STEPS_SOFTMAX):
                        project(b + 1, k)
                for n in range(NAV):
                    av_sum(b, n, follows)
                    if follows and n in step_after:
                        project(b + 1, step_after[n])

            pe.wait_ge(ident_ready, 2)
            pe.wait_ge(weights_in, 16 * (3 * 2 + 4 * TRI + 2))
            pe.wait_ge(w1_steps, 8 + 3 * 4)
            for k in range(len(STEPS)):
                project(0, k)
            block_work(0, False, True)
            with pe.Fori(1, NBLK - 1) as b:
                block_work(b, True, True)
            block_work(NBLK - 1, True, False)
            for n in range(MLP_STEPS):
                mlp(NBLK - 1, n, False)


def kernel(x, L0_conv_w_qkv, L0_conv_pos_embedding, L0_conv_w1, L0_conv_b1, L0_conv_ln_g, L0_conv_ln_b, L0_conv_w2,
           L0_conv_b2):
    import numpy as np
    import concourse.bacc as bacc
    from concourse.bass_utils import run_bass_kernel_spmd

    HEADS, HD = 4, 16
    C = HEADS * HD
    w = np.asarray(L0_conv_w_qkv).reshape(3, HEADS, HD, C).transpose(3, 0, 2, 1).reshape(C, 3 * C)
    arrays = {
        "x": np.ascontiguousarray(x),
        "w_qk_t": np.ascontiguousarray(w[:, :2 * C]),
        "w_v_t": np.ascontiguousarray(w[:, 2 * C:]),
        "pos": np.ascontiguousarray(L0_conv_pos_embedding),
        "w1_t": np.ascontiguousarray(np.asarray(L0_conv_w1).T),
        "b1": np.ascontiguousarray(L0_conv_b1),
        "ln_g": np.ascontiguousarray(L0_conv_ln_g),
        "ln_b": np.ascontiguousarray(L0_conv_ln_b),
        "w2_t": np.ascontiguousarray(np.asarray(L0_conv_w2).T),
        "b2": np.ascontiguousarray(L0_conv_b2),
    }
    nc = bacc.Bacc("TRN2", target_bir_lowering=False, num_devices=1)
    args = [nc.dram_tensor(f"in_{n}", a.shape, mybir.dt.float32, kind="ExternalInput").ap() for n, a in arrays.items()]
    out = nc.dram_tensor("out_y", arrays["x"].shape, mybir.dt.float32, kind="ExternalOutput").ap()
    build_windowed_attention(nc, *args, out)
    r = run_bass_kernel_spmd(nc, [{f"in_{n}": a for n, a in arrays.items()}], core_ids=[0])
    return r.results[0]["out_y"]
```
